# Optimizing a Trainium2 kernel written in Bass

```python
import numpy as np
import jax
import jax.numpy as jnp

def _softmax(x, axis=-1):
    return jax.nn.softmax(x, axis=axis)
def _gelu(x):
    return jax.nn.gelu(x, approximate=True)
def _silu(x):
    return jax.nn.silu(x)
def _sigmoid(x):
    return jax.nn.sigmoid(x)
def _layernorm(x, axis=-1, eps=1e-5):
    m = jnp.mean(x, axis=axis, keepdims=True)
    v = jnp.var(x, axis=axis, keepdims=True)
    return (x - m) / jnp.sqrt(v + eps)
def _scatter_add(tgt, idx, src, axis=0):
    return tgt.at[idx].add(src)
def _segment_sum(src, seg, n):
    return jax.ops.segment_sum(src, seg, n)

kernel_name = 'mk_conv_preact_d2_conv_nhwc64_15ab5e'

def setup_inputs(seed: int = 0):
    np.random.seed(seed)
    _w = jnp.asarray
    def _rec_inputs():
        import jax
        import jax.numpy as jnp
        _gk = jax.random.key(seed)
        x = -7.109e-05 + 0.9999 * jax.random.normal(jax.random.fold_in(_gk, 1), (4, 512, 512, 64), jnp.float32)
        return x
    x = _rec_inputs()
    def _L0_conv_setup():
        import jax, jax.numpy as jnp
        import numpy as np
        PS = 8
        NUM_HEADS = 4
        key = jax.random.key(seed)
        ks = jax.random.split(key, 6)
        t, h, w, c = (4, 512, 512, 64)
        vid = jax.random.normal(ks[0], (t, h, w, c), dtype=jnp.float32)
        modulator = jax.random.normal(ks[1], (PS * PS, c), dtype=jnp.float32) * 0.02
        w_qkv = jax.random.normal(ks[2], (3 * c, c), dtype=jnp.float32) * c ** (-0.5)
        b_qkv = jax.random.normal(ks[3], (3 * c,), dtype=jnp.float32) * 0.02
        w_proj = jax.random.normal(ks[4], (c, c), dtype=jnp.float32) * c ** (-0.5)
        b_proj = jax.random.normal(ks[5], (c,), dtype=jnp.float32) * 0.02
        return {'vid': vid, 'modulator': modulator, 'w_qkv': w_qkv, 'b_qkv': b_qkv, 'w_proj': w_proj, 'b_proj': b_proj}
    _L0_conv_all = _L0_conv_setup()
    _L0_conv_in = {k: v for k, v in _L0_conv_all.items() if k in ('modulator', 'w_qkv', 'b_qkv', 'w_proj', 'b_proj', )}
    del _L0_conv_all

    def _L1_conv_setup():
        import jax, jax.numpy as jnp
        import numpy as np
        B, H, W_SP, C_IN, C_OUT = (8, 256, 256, 64, 64)
        MODES = (32, 32)
        M1, M2 = (MODES[0], MODES[1] // 2 + 1)
        key = jax.random.key(seed)
        k1, k2, k3 = jax.random.split(key, 3)
        scale = 1.0 / C_IN
        x = jax.random.normal(k1, (B, H, W_SP, C_IN), dtype=jnp.float32)
        W_real = scale * jax.random.normal(k2, (M1, M2, C_IN, C_OUT), dtype=jnp.float32)
        W_imag = scale * jax.random.normal(k3, (M1, M2, C_IN, C_OUT), dtype=jnp.float32)
        return {'x': x, 'W_real': W_real, 'W_imag': W_imag}
    _L1_conv_all = _L1_conv_setup()
    _L1_conv_in = {k: v for k, v in _L1_conv_all.items() if k in ('W_real', 'W_imag', )}
    del _L1_conv_all

    return {
        "x": x,
        "L0_conv_modulator": _L0_conv_in["modulator"],
        "L0_conv_w_qkv": _L0_conv_in["w_qkv"],
        "L0_conv_b_qkv": _L0_conv_in["b_qkv"],
        "L0_conv_w_proj": _L0_conv_in["w_proj"],
        "L0_conv_b_proj": _L0_conv_in["b_proj"],
        "L1_conv_W_real": _L1_conv_in["W_real"],
        "L1_conv_W_imag": _L1_conv_in["W_imag"],
    }

def reference(x, L0_conv_modulator, L0_conv_w_qkv, L0_conv_b_qkv, L0_conv_w_proj, L0_conv_b_proj, L1_conv_W_real, L1_conv_W_imag):
    import jax
    import jax.numpy as jnp
    def _L0_conv_ref(vid, modulator, w_qkv, b_qkv, w_proj, b_proj):
        import jax, jax.numpy as jnp
        import numpy as np
        PS = 8
        NUM_HEADS = 4
        t, h, w, c = vid.shape
        hd = c // NUM_HEADS
        scale = hd ** (-0.5)
        nh, nw = (h // PS, w // PS)
        x = vid.reshape(t, nh, PS, nw, PS, c)
        x = x.transpose(0, 1, 3, 2, 4, 5).reshape(t * nh * nw, PS * PS, c)
        x = x + modulator[None]
        qkv = jnp.einsum('bnc,dc->bnd', x, w_qkv) + b_qkv
        q, k, v = jnp.split(qkv, 3, axis=-1)
        B, N, _ = q.shape
        q = q.reshape(B, N, NUM_HEADS, hd).transpose(0, 2, 1, 3) * scale
        k = k.reshape(B, N, NUM_HEADS, hd).transpose(0, 2, 1, 3)
        v = v.reshape(B, N, NUM_HEADS, hd).transpose(0, 2, 1, 3)
        attn = jnp.einsum('bhnd,bhmd->bhnm', q, k)
        attn = jax.nn.softmax(attn, axis=-1)
        out = jnp.einsum('bhnm,bhmd->bhnd', attn, v)
        out = out.transpose(0, 2, 1, 3).reshape(B, N, c)
        out = jnp.einsum('bnc,dc->bnd', out, w_proj) + b_proj
        out = out.reshape(t, nh, nw, PS, PS, c).transpose(0, 1, 3, 2, 4, 5)
        return out.reshape(t, h, w, c)

    def _L1_conv_ref(x, W_real, W_imag):
        import jax, jax.numpy as jnp
        import numpy as np
        B, H, W_SP, C_IN, C_OUT = (8, 256, 256, 64, 64)
        MODES = (32, 32)
        M1, M2 = (MODES[0], MODES[1] // 2 + 1)
        b, h, w, c_in = x.shape
        m1, m2, _, c_out = W_real.shape
        xc = jnp.transpose(x, (0, 3, 1, 2))
        spec = jnp.fft.rfftn(xc, axes=(-2, -1), norm='forward')
        spec_sh = jnp.fft.fftshift(spec, axes=(-2,))
        start1 = h - m1
        r0 = start1 // 2
        xs = spec_sh[:, :, r0:r0 + m1, :m2]
        Wc = (W_real + 1j * W_imag).astype(spec.dtype)
        conv_modes = jnp.einsum('bimn,mnio->bomn', xs, Wc)
        conv = jnp.zeros((b, c_out, h, w // 2 + 1), dtype=spec.dtype)
        conv = conv.at[:, :, r0:r0 + m1, :m2].set(conv_modes)
        conv = jnp.fft.ifftshift(conv, axes=(-2,))
        y = jnp.fft.irfftn(conv, s=(h, w), axes=(-2, -1), norm='forward')
        return jnp.transpose(y, (0, 2, 3, 1))

    def _gn(v, G=32, eps=1e-5):
        B_, H_, W_, C_ = v.shape
        g = v.reshape(B_, H_, W_, G, C_ // G)
        m = jnp.mean(g, axis=(1, 2, 4), keepdims=True)
        s = jnp.var(g, axis=(1, 2, 4), keepdims=True)
        return ((g - m) / jnp.sqrt(s + eps)).reshape(v.shape)

    def _ln_c(v, eps=1e-6):
        m = jnp.mean(v, axis=-1, keepdims=True)
        s = jnp.var(v, axis=-1, keepdims=True)
        return (v - m) / jnp.sqrt(s + eps)

    def _ln_t(v, eps=1e-5):
        m = jnp.mean(v, axis=-1, keepdims=True)
        s = jnp.var(v, axis=-1, keepdims=True)
        return (v - m) / jnp.sqrt(s + eps)

    def _to_tokens(v):
        B_, H_, W_, C_ = v.shape
        return v.reshape(B_, H_ * W_, C_)
    def _from_tokens(t, like):
        return t.reshape(like.shape)

    x = x + _L0_conv_ref(_gn(x), L0_conv_modulator, L0_conv_w_qkv, L0_conv_b_qkv, L0_conv_w_proj, L0_conv_b_proj)
    x = x + _L1_conv_ref(_gn(x), L1_conv_W_real, L1_conv_W_imag)
    return x


_drawn_inputs = setup_inputs


def setup_inputs(seed=0):
    import zlib

    import numpy as np

    out = dict(_drawn_inputs(seed))
    spreads = {}
    factors = {'L0_conv_modulator': 7.507,
     'L0_conv_b_qkv': 3.624,
     'L1_conv_W_real': 5.349,
     'L1_conv_W_imag': 5.498}
    for name, (base, spread) in spreads.items():
        noise = np.random.default_rng([zlib.crc32(name.encode()), seed]).standard_normal(out[name].shape)
        drawn = base * np.exp(spread * noise) if base else spread * noise
        out[name] = jnp.asarray(drawn.astype(out[name].dtype))
    for name, factor in factors.items():
        out[name] = (out[name] * factor).astype(out[name].dtype)
    return out
```

```python
from contextlib import ExitStack

import numpy as np

import concourse.bass as bass
from concourse import mybir

F32 = mybir.dt.float32
F32R = mybir.dt.float32r
ACT = mybir.ActivationFunctionType
ALU = mybir.AluOpType
AX = mybir.AxisListType

C = 64
W = 512
P = 128
NH = 4
HD = C // NH
PS = 8
N = PS * PS
M1, M2 = 32, 17
KW = 2 * M2
E = 128
WP = W // (2 * PS)
CH = 4
NC = WP // CH
ROW = PS * 2 * E
GRP = 4
NG = 2 * PS // GRP
RING = 4
EPS = 1e-5


def tables(H):
    p = np.arange(P)
    t = {}
    wpix = (256 * np.arange(2)[:, None] + np.arange(2)[None, :])[None] + 2 * p[:, None, None]
    ang = 2 * np.pi * ((wpix[..., None] * np.arange(M2)) % W) / W
    t["fwd_w"] = (np.concatenate([np.cos(ang), -np.sin(ang)], -1) / W).reshape(P, 4 * KW)
    kh = np.arange(M1) - M1 // 2
    h = np.arange(H)
    ang = 2 * np.pi * ((h[:, None] * kh) % H) / H
    c, s = np.cos(ang) / H, np.sin(ang) / H
    fwd_h = np.stack([np.concatenate([c, -s], 1), np.concatenate([s, c], 1)], 1)
    hp = min(P, H)
    t["fwd_h"] = fwd_h.reshape(H // hp, hp, 2, 2 * M1).transpose(1, 0, 2, 3).reshape(hp, -1)
    c, s = np.cos(ang).T, np.sin(ang).T
    t["inv_h"] = np.concatenate([c, -s, s, c], 0)
    a = np.where(np.arange(M2) == 0, 1.0, 2.0)[:, None]
    wpix = (4 * p[None, :] + np.arange(4)[:, None]).reshape(-1)
    ang = 2 * np.pi * ((np.arange(M2)[:, None] * wpix) % W) / W
    t["inv_w"] = np.concatenate([a * np.cos(ang), -a * np.sin(ang)], 0)
    t["ident"] = np.eye(P)
    t["token_eye"] = np.concatenate([np.eye(N), np.eye(N)], 0)
    t["head_mask"] = ((p[:, None] % C) // HD == np.arange(NH)).astype(float)
    t["half_mask"] = (p[:, None] // C == np.arange(2)).astype(float)
    same = (p[:, None] // C) == (p[None, :] // C)
    t["neg_same_window"] = -same.astype(float)
    t["group_avg"] = (((p[:, None] % C) // 2) == ((p[None, :] % C) // 2)) / (2.0 * H * W)
    t["group_mean2"] = (same & ((p[:, None] // 2) == (p[None, :] // 2))) / 2.0
    z, i = np.zeros((M1, M1)), np.eye(M1)
    t["mode_parts"] = np.concatenate([np.eye(2 * M1), np.block([[z, i], [-i, z]])], 1)
    return {k: np.ascontiguousarray(v, np.float32) for k, v in t.items()}


class Place:

    def __init__(self, strips, img, quad, j, known=None):
        self.strips, self.img, self.quad, self.j, self.known = strips, img, quad, j, known

    def index(self, off=0, per=1):
        return self.img * (self.strips // per) + self.quad * (RING // per) + (self.j + off) // per

    def strip(self, off=0):
        return self.quad * RING + (self.j + off)


def wait_item(eng, sem, at, off, per, n):
    if at.known is None or per * (at.known + off) + n > 0:
        eng.wait_ge(sem, at.index(off) * per + n)


def wait_apart(eng, sem, value, passed):
    eng.wait_ge(sem, value).then_inc(passed, 1)


def wait_item_apart(eng, sem, at, off, per, n, passed):
    if at.known is None or per * (at.known + off) + n > 0:
        wait_apart(eng, sem, at.index(off) * per + n, passed)


def program(nc, ext, out, IMG, H):
    S = H // PS
    ctx = ExitStack()
    with ctx:
        def sb(stack, name, shape, dt=F32):
            return stack.enter_context(nc.sbuf_tensor(name, shape, dt))

        x1 = nc.dram_tensor("x1", [IMG * H, W * C], F32, kind="Internal").ap()
        y1 = nc.dram_tensor("y1", [IMG, KW, H * C], F32, kind="Internal").ap()

        stats1 = sb(ctx, "stats1", [P, IMG, 3])
        sqsum = sb(ctx, "sqsum", [P, IMG])
        ones = sb(ctx, "ones", [P, 1])
        group_avg = sb(ctx, "group_avg", [P, P])
        pass1(nc, ext, stats1, ones, group_avg, IMG, S)
        pass2(nc, ext, x1, y1, stats1, sqsum, ones, IMG, S)
        with ExitStack() as late:
            back = sb(late, "back", [P, IMG, C, KW])
            pass3(nc, ext, y1, sqsum, group_avg, back, IMG, H)
            pass4(nc, ext, x1, back, out, IMG, H)


def pass1(nc, ext, stats1, ones, group_avg, IMG, S):
    TB = 4
    PE_PARTS = 3
    Q = ROW // 4
    xt = ext["x"].rearrange("(t r) e -> t (r e)", r=PS).rearrange("t (p f) -> t p f", p=P)
    with ExitStack() as c:
        sb = lambda n, shape: c.enter_context(nc.sbuf_tensor(n, shape, F32))
        tile = sb("p1_x", [P, TB, ROW])
        sq = sb("p1_sq", [P, 2, ROW])
        sum_sq = sb("p1_sum_sq", [P, ROW])
        sum_x = sb("p1_sum_x", [P, Q])
        zero = sb("p1_zero", [P, Q])
        row = sb("p1_row", [1, Q])
        part = sb("p1_part", [P, 2])
        work = sb("p1_work", [P, 3])
        row_ps = c.enter_context(nc.psum_tensor("p1_row_ps", [P, Q], F32))
        part_ps = c.enter_context(nc.psum_tensor("p1_part_ps", [P, Q], F32))
        avg_ps = c.enter_context(nc.psum_tensor("p1_avg_ps", [P, Q], F32))
        sem = lambda n: c.enter_context(nc.semaphore(n))
        loaded = [sem(f"p1_loaded{i}") for i in range(TB)]
        consts, set_up, zeroed = sem("p1_consts"), sem("p1_set_up"), sem("p1_zeroed")
        pe_summed = sem("p1_pe_summed")
        sq_done = sem("p1_sq_done")
        sq_free = sem("p1_sq_free")
        x_summed = sem("p1_x_summed")
        pe_row, row_out = sem("p1_pe_row"), sem("p1_row_out")
        parts, parts_out, avg = sem("p1_parts"), sem("p1_parts_out"), sem("p1_avg")
        chain, dev = sem("p1_chain"), sem("p1_dev")
        passed = sem("p1_passed")
        CHAIN = 4
        block = c.enter_context(nc.Block())

        @block.sync
        def _(sp):
            sp.dma_start(group_avg[:], ext["group_avg"]).then_inc(consts, 16)
            for t in range(TB):
                sp.dma_start(tile[:, t, :], xt[t]).then_inc(loaded[t], 16)
            with sp.Fori(0, IMG * S // TB - 1) as i:
                for t in range(TB):
                    wait_apart(sp, pe_summed, i * TB + (t + 1), passed)
                    wait_apart(sp, sq_done, i * TB + (t + 1), passed)
                    sp.wait_ge(x_summed, i * TB + (t + 2))
                    sp.dma_start(tile[:, t, :], xt[i * TB + (TB + t)]).then_inc(loaded[t], 16)

        @block.tensor
        def _(pe):
            pe.wait_ge(set_up, 2)
            pe.wait_ge(consts, 16)
            for img in range(IMG):
                nc.tensor.matmul(row_ps[0:1, :], ones[:], zero[:], start=True, stop=False)
                with pe.Fori(0, S // TB) as i:
                    for t in range(TB):
                        pe.wait_ge(loaded[t], (i + (img * (S // TB) + 1)) * 16)
                        for q in range(PE_PARTS):
                            last = nc.tensor.matmul(row_ps[0:1, :], ones[:], tile[:, t, q * Q:(q + 1) * Q],
                                                    start=False, stop=False)
                        last.then_inc(pe_summed, 1)
                nc.tensor.matmul(row_ps[0:1, :], ones[:], zero[:], start=False, stop=True).then_inc(pe_row, 1)
                pe.wait_ge(row_out, img + 1)
                pe.wait_ge(x_summed, (img + 1) * S + 1)
                pe.wait_ge(sq_free, (img + 1) * S + 2)
                for k in range(Q // P):
                    nc.tensor.matmul(part_ps[:, 0:1], row[0:1, k * P:(k + 1) * P], ones[0:1, :],
                                     start=(k == 0), stop=False)
                for k in range(Q // P):
                    nc.tensor.matmul(part_ps[:, 0:1], sum_x[:, k * P:(k + 1) * P], ones[:],
                                     start=False, stop=(k == Q // P - 1))
                for k in range(ROW // P):
                    last = nc.tensor.matmul(part_ps[:, 1:2], sum_sq[:, k * P:(k + 1) * P], ones[:],
                                            start=(k == 0), stop=(k == ROW // P - 1))
                last.then_inc(parts, 1)
                pe.wait_ge(parts_out, img + 1)
                nc.tensor.matmul(avg_ps[:, 0:2], group_avg[:], part[:], start=True, stop=True).then_inc(avg, 1)

        @block.scalar
        def _(act):
            for img in range(IMG):
                with act.Fori(0, S // TB) as i:
                    for t in range(TB):
                        act.wait_ge(loaded[t], (i + (img * (S // TB) + 1)) * 16)
                        act.wait_ge(sq_free, i * TB + (img * S + t + 1))
                        nc.scalar.activation(sq[:, t % 2, :], tile[:, t, :], ACT.Square).then_inc(sq_done, 1)
                act.wait_ge(pe_row, img + 1)
                nc.scalar.activation(row[:], row_ps[0:1, :], ACT.Copy).then_inc(row_out, 1)
                act.wait_ge(chain, CHAIN * img + CHAIN - 1)
                nc.scalar.activation(stats1[:, img, 1:2], work[:, 2:3], ACT.Sqrt).then_inc(dev, 1)

        @block.vector
        def _(dve):
            nc.vector.memset(ones[:], 1.0).then_inc(set_up, 1)
            nc.vector.memset(zero[:], 0.0).then_inc(set_up, 1)
            nc.vector.memset(sq[:], 0.0).then_inc(sq_free, 2)
            nc.vector.memset(part[:], 0.0).then_inc(x_summed, 1)
            for img in range(IMG):
                nc.vector.memset(sum_sq[:], 0.0).then_inc(zeroed, 1)
                nc.vector.memset(sum_x[:], 0.0).then_inc(zeroed, 1)
                dve.wait_ge(zeroed, 2 * (img + 1))
                with dve.Fori(0, S // TB) as i:
                    for t in range(TB):
                        n = img * S + t
                        dve.wait_ge(sq_done, i * TB + (n + 1))
                        dve.wait_ge(sq_free, i * TB + (n + 2))
                        nc.vector.tensor_tensor(sum_sq[:], sum_sq[:], sq[:, t % 2, :], ALU.add).then_inc(sq_free, 1)
                        dve.wait_ge(x_summed, i * TB + (n + 1))
                        nc.vector.tensor_tensor(sum_x[:], sum_x[:], tile[:, t, PE_PARTS * Q:], ALU.add)\
                            .then_inc(x_summed, 1)
                dve.wait_ge(parts, img + 1)
                nc.vector.tensor_copy(part[:], part_ps[:, 0:2]).then_inc(parts_out, 1)
                dve.wait_ge(avg, img + 1)
                group_stats(nc, dve, stats1[:, img, :], avg_ps, work, chain, CHAIN * img, dev, img)


def group_stats(nc, dve, stats, avg_ps, work, chain, steps, dev, devs):
    nc.vector.tensor_copy(stats[:, 0:1], avg_ps[:, 0:1]).then_inc(chain, 1)
    dve.wait_ge(chain, steps + 1)
    nc.vector.tensor_tensor(work[:, 0:1], avg_ps[:, 0:1], stats[:, 0:1], ALU.mult).then_inc(chain, 1)
    dve.wait_ge(chain, steps + 2)
    nc.vector.tensor_tensor(work[:, 1:2], avg_ps[:, 1:2], work[:, 0:1], ALU.subtract).then_inc(dev, 1)
    dve.wait_ge(dev, 2 * devs + 1)
    nc.vector.tensor_scalar(work[:, 2:3], work[:, 1:2], 0.0, EPS, ALU.max, ALU.add).then_inc(chain, 1)
    dve.wait_ge(dev, 2 * devs + 2)
    nc.vector.reciprocal(stats[:, 2:3], stats[:, 1:2]).then_inc(chain, 1)
    dve.wait_ge(chain, steps + 4)


def pass2(nc, ext, x1, y1, stats1, sqsum, ones, IMG, S):
    UP = 2
    UN = CH // UP
    NU = NC * UN
    strips = lambda a: a.rearrange("(g r) (ab p i c) -> g ab p r i c", r=PS, ab=2, p=P, i=2)
    xv, x1v = strips(ext["x"]), strips(x1)
    PARTS = [(i2, ab) for i2 in range(2) for ab in range(2)]
    y1v = y1.rearrange("i k (s e) -> i s k e", e=PS * C)
    with ExitStack() as c:
        sb = lambda n, shape, dt=F32: c.enter_context(nc.sbuf_tensor(n, shape, dt))
        xs = sb("xs", [P, RING, PS, 2, 2, C])
        xt = sb("xt", [P, 2, WP, N])
        q_sb = sb("q_sb", [P, 2, CH, N])
        k_sb = sb("k_sb", [P, 2, CH, N])
        k_heads = sb("k_heads", [P, 2, CH, NH, N], F32R)
        q_diag = sb("q_diag", [P, 2, CH, P], F32R)
        q_heads = sb("q_heads", [P, 4, CH, NH, N])
        k_diag = sb("k_diag", [P, 4, CH, P])
        v_diag = sb("v_diag", [P, 2, CH, P])
        v_ones = sb("v_ones", [P, 4, CH, 2, P])
        peak = sb("peak", [P, 2, UP * NH])
        peak_diag = sb("peak_diag", [P, 4, UP, NH, N], F32R)
        probs = sb("probs", [P, 4, UP, NH, N])
        log_sum = sb("log_sum", [P, 2, UP, 2, N])
        inv_sum = sb("inv_sum", [P, 2, UP, 2, N])
        heads = sb("heads", [P, 2, 2, 2 * PS, WP, 4])
        sq = sb("sq", [P, 4, ROW // 4])
        sum_sq = sb("sum_sq", [P, 4, ROW // 4])
        width_modes = sb("width_modes", [KW, 2, PS * C])
        w_in = sb("w_in", [P, 3, P])
        b_in = sb("b_in", [P, 3])
        w_cur = sb("w_cur", [P, 3, P])
        b_q = sb("b_q", [P, 1])
        mod = sb("mod", [P, N])
        mod_cur = sb("mod_cur", [P, N])
        w_out = sb("w_out", [P, 2, P])
        b_rows = sb("b_rows", [1, 2, 512])
        b_lo = sb("b_lo", [1, 512])
        b_out = sb("b_out", [64, 512], F32R)
        ones_r = sb("ones_r", [64, P], F32R)
        fwd_w = sb("fwd_w", [P, 4, KW])
        ident = sb("ident", [P, P])
        token_eye = sb("token_eye", [P, N])
        head_mask = sb("head_mask", [P, NH])
        half_mask = sb("half_mask", [P, 2])
        neg_same = sb("neg_same", [P, P])
        neg_same_r = sb("neg_same_r", [P, P], F32R)
        bank = lambda n: c.enter_context(nc.psum_tensor(n, [P, 512], F32))
        qk_bank, mix_bank, out_bank, peak_bank = bank("qk_bank"), bank("mix_bank"), bank("out_bank"), bank("peak_bank")
        score_bank = [bank(f"score_bank{i}") for i in range(2)]
        value_bank = [bank(f"value_bank{i}") for i in range(2)]
        sem = lambda n: c.enter_context(nc.semaphore(n))
        consts, zeroed, img_set = sem("consts"), sem("zeroed"), sem("img_set")
        loaded = [sem(f"loaded{i}") for i in range(RING)]
        stored = [sem(f"stored{i}") for i in range(RING)]
        y_stored = [sem(f"y_stored{i}") for i in range(2)]
        xt_ps, xt_ok = sem("xt_ps"), sem("xt_ok")
        qk_ps, qk_ok = sem("qk_ps"), sem("qk_ok")
        v_ps, vd_ok = sem("v_ps"), sem("vd_ok")
        vt_ps, vo_ok = sem("vt_ps"), sem("vo_ok")
        ops1_ok, ops2_ok = sem("ops1_ok"), sem("ops2_ok")
        peak_ps, peak_ok, pd_ok = sem("peak_ps"), sem("peak_ok"), sem("pd_ok")
        score_ps, probs_ok = sem("score_ps"), sem("probs_ok")
        value_ps, log_ok, inv_ok, heads_ok = sem("value_ps"), sem("log_ok"), sem("inv_ok"), sem("heads_ok")
        out_ps, x1_ok = sem("out_ps"), sem("x1_ok")
        y_ps, y_ok = sem("y_ps"), sem("y_ok")
        sq_ok, sum_ok = sem("sq_ok"), sem("sum_ok")
        sum_ps, img_done = sem("sum_ps"), sem("img_done")
        passed = sem("passed")
        joined = sem("joined")
        block = c.enter_context(nc.Block())

        def live(at, off, n=0, per=NC):
            return at.known is None or 0 <= per * (at.known + off) + n < per * S

        def sweep(eng, img, body, straight=0):
            for s in range(RING):
                body(Place(S, img, 0, s, known=s))
            if S // RING - straight // RING > 1:
                with eng.Fori(1, (S - straight) // RING) as quad:
                    for j in range(RING):
                        body(Place(S, img, quad, j))
            for s in range(max(S - straight, RING), S + 3):
                body(Place(S, img, s // RING, s % RING, known=s))

        def join(eng, img):
            wait_apart(eng, img_done, img + 1, joined)
            for i in range(RING):
                wait_apart(eng, stored[i], (img + 1) * (64 * (S // RING)), joined)
            for i in range(2):
                wait_apart(eng, y_stored[i], (img + 1) * (16 * (S // 2)), joined)

        @block.sync
        def _(sp):
            for dst, name in ((w_in, "w_in"), (b_in, "b_in"), (mod, "mod"), (w_out, "w_out"), (b_rows, "b_out"),
                              (fwd_w, "fwd_w"), (ident, "ident"), (token_eye, "token_eye"),
                              (head_mask, "head_mask"), (half_mask, "half_mask"), (neg_same, "neg_same_window")):
                sp.dma_start(dst[:], ext[name]).then_inc(consts, 16)

            def load(strip, slot):
                for i2, ab in PARTS:
                    sp.dma_start(xs[:, slot, :, i2, ab, :], xv[strip, ab, :, :, i2, :]).then_inc(loaded[slot], 16)

            def body(at):
                if live(at, -3):
                    wait_item(sp, y_ok, at, -3, 1, 1)
                    slot = (at.j - 3) % 2
                    sp.dma_start(y1v[at.img, at.strip(-3)], width_modes[:, slot, :]).then_inc(y_stored[slot], 16)
                if live(at, 1):
                    slot = (at.j + 1) % RING
                    if at.known is None or at.known >= RING - 1:
                        wait_item(sp, y_ps, at, -3, 1, 1)
                        wait_item(sp, sq_ok, at, -3, 4, 4)
                        sp.wait_ge(stored[slot], (at.index(-3, RING) + 1) * 64)
                    load(at.index(1), slot)
                if live(at, -2):
                    wait_item(sp, x1_ok, at, -2, 4, 4)
                    slot = (at.j - 2) % RING
                    for i2, ab in PARTS:
                        sp.dma_start(x1v[at.index(-2), ab, :, :, i2, :], xs[:, slot, :, i2, ab, :]).then_inc(stored[slot], 16)

            with sp.Fori(0, IMG) as img:
                load(img * S, 0)
                sweep(sp, img, body, straight=RING)
                join(sp, img)

        @block.tensor
        def _(pe):
            wq, wk, wv = (w_cur[:, i, :] for i in range(3))

            def peak_scores(at, t, u):
                if not live(at, -1, t):
                    return
                wait_item(pe, ops1_ok, at, -1, NC, t + 1)
                wait_item(pe, peak_ok, at, -1, NU, UN * t + u)
                for j in range(UP):
                    pair = UP * u + j
                    last = nc.tensor.matmul(peak_bank[:, j * 256:(j + 1) * 256], q_diag[:, t % 2, pair, :],
                                            k_heads[:, t % 2, pair].rearrange("p h n -> p (h n)"),
                                            start=True, stop=True)
                last.then_inc(peak_ps, 1)

            def scores(at, t, u):
                if not live(at, -1, t):
                    return
                unit = UN * t + u
                ps = score_bank[u]
                wait_item(pe, pd_ok, at, -1, NU, unit + 1)
                wait_item(pe, ops2_ok, at, -1, NC, t + 1)
                wait_item(pe, probs_ok, at, -1, NU, unit - 1)
                nc.tensor.matmul(ps[:], neg_same_r[:], peak_diag[:, unit % 4].rearrange("p a h n -> p (a h n)"),
                                 start=True, stop=False)
                for j in range(UP):
                    pair = UP * u + j
                    last = nc.tensor.matmul(ps[:, j * 256:(j + 1) * 256], k_diag[:, t % 4, pair, :],
                                            q_heads[:, t % 4, pair].rearrange("p h n -> p (h n)"),
                                            start=False, stop=(j == UP - 1))
                last.then_inc(score_ps, 1)

            def values(at, t, u):
                if not live(at, -1, t):
                    return
                unit = UN * t + u
                wait_item(pe, probs_ok, at, -1, NU, unit + 1)
                wait_item(pe, vo_ok, at, -1, NC, t + 1)
                wait_item(pe, heads_ok, at, -1, NU, unit - 1)
                for j in range(UP):
                    for g in range(2):
                        o = (2 * j + g) * P
                        last = nc.tensor.matmul(
                            value_bank[u][:, o:o + P], v_ones[:, t % 4, UP * u + j, g, :],
                            probs[:, unit % 4, j, 2 * g:2 * g + 2, :].rearrange("p h n -> p (h n)"),
                            start=True, stop=True)
                last.then_inc(value_ps, 1)

            def tick(at, c):
                src = xt[:, (at.j - 1) % 2, CH * c:CH * (c + 1), :].rearrange("p w n -> p (w n)")
                if live(at, -1, c):
                    wait_item(pe, xt_ok, at, -1, NG, NG)
                    wait_item(pe, qk_ok, at, -1, NC, c)
                    nc.tensor.matmul(qk_bank[:, 0:256], wq, src, start=True, stop=True)
                    nc.tensor.matmul(qk_bank[:, 256:512], wk, src, start=True, stop=True).then_inc(qk_ps, 1)
                peak_scores(at, c - 1, 0)
                scores(at, c - 2, 0)
                if live(at, -1, c):
                    wait_item(pe, vd_ok, at, -1, NC, c)
                    wait_item(pe, xt_ok, at, 0, NG, c // 2 if live(at, 0) else 0)
                    nc.tensor.matmul(mix_bank[:, 0:256], wv, src, start=True, stop=True).then_inc(v_ps, 1)
                values(at, c - 3, 0)
                peak_scores(at, c - 1, 1)
                if live(at, -1, c):
                    wait_item(pe, vd_ok, at, -1, NC, c + 1)
                    wait_item(pe, vo_ok, at, -1, NC, c)
                    if live(at, -2):
                        wait_item(pe, x1_ok, at, -2, NG, max(c - 4, 0))
                    if c >= 2 and live(at, -3):
                        wait_item(pe, y_ok, at, -3, 1, 1)
                    for j in range(CH):
                        last = nc.tensor.transpose(out_bank[:, j * P:(j + 1) * P], v_diag[:, c % 2, j, :], ident[:])
                    last.then_inc(vt_ps, 1)
                scores(at, c - 2, 1)
                values(at, c - 3, 1)
                if c % 2 and live(at, 0):
                    g = c // 2
                    if g == 0:
                        pe.wait_ge(loaded[at.j], (at.index(0, RING) + 1) * 64)
                    if live(at, -1):
                        wait_item(pe, vd_ok, at, -1, NC, c + 1)
                    wait_item(pe, xt_ok, at, 0, NG, g)
                    for i in range(GRP):
                        r, i2 = 2 * g + i // 2, i % 2
                        last = nc.tensor.transpose(mix_bank[:, i * P:(i + 1) * P],
                                                   xs[:, at.j, r, i2].rearrange("p a c -> p (a c)"), ident[:])
                    last.then_inc(xt_ps, 1)
                if c == 1 and live(at, -3):
                    wait_item(pe, x1_ok, at, -3, NG, NG)
                    if live(at, -1):
                        wait_item(pe, vo_ok, at, -1, NC, c + 1)
                    for i in range(4):
                        ab, i2 = i // 2, i % 2
                        last = nc.tensor.matmul(out_bank[0:KW, :], fwd_w[:, i, :],
                                                xs[:, (at.j - 3) % RING, :, i2, ab, :],
                                                start=(i == 0), stop=(i == 3))
                    last.then_inc(y_ps, 1)
                if c >= 4 and live(at, -2):
                    g = c - 4
                    wait_item(pe, heads_ok, at, -2, NU, NU)
                    wait_item(pe, x1_ok, at, -2, NG, g)
                    if live(at, -1):
                        wait_item(pe, vo_ok, at, -1, NC, c + 1)
                    nc.tensor.matmul(out_bank[:], ones_r[:], b_out[:], start=True, stop=False)
                    for i in range(GRP):
                        for h2 in range(2):
                            tok = heads[:, (at.j - 2) % 2, h2, GRP * g + i].rearrange("p w j -> p (w j)")
                            last = nc.tensor.matmul(out_bank[:, i * P:(i + 1) * P], tok, w_out[:, h2, :],
                                                    start=False, stop=(i == GRP - 1 and h2 == 1))
                    last.then_inc(out_ps, 1)

            def body(at):
                for c in range(NC):
                    tick(at, c)

            pe.wait_ge(consts, 176)
            pe.wait_ge(zeroed, ZEROED)
            with pe.Fori(0, IMG) as img:
                pe.wait_ge(img_set, (img + 1) * SET_STEPS)
                sweep(pe, img, body)
                pe.wait_ge(sum_ok, (img + 1) * (NG * S))
                pe.wait_ge(y_ok, (img + 1) * S)
                for k in range(ROW // P):
                    last = nc.tensor.matmul(out_bank[:, 0:1], sum_sq[:].rearrange("p a b -> p (a b)")[:, k * P:(k + 1) * P],
                                            ones[:], start=(k == 0), stop=(k == ROW // P - 1))
                last.then_inc(sum_ps, 1)
                join(pe, img)

        @block.scalar
        def _(act):
            def exponentials(at, t, u):
                if not live(at, -1, t):
                    return
                unit = UN * t + u
                wait_item(act, score_ps, at, -1, NU, unit + 1)
                wait_item(act, value_ps, at, -1, NU, unit - 3)
                nc.scalar.activation(probs[:, unit % 4].rearrange("p a h n -> p (a h n)"), score_bank[u][:], ACT.Exp)\
                    .then_inc(probs_ok, 1)

            def inverse_sums(at, t, u):
                if not live(at, -1, t):
                    return
                unit = UN * t + u
                wait_item(act, value_ps, at, -1, NU, unit + 1)
                wait_item(act, inv_ok, at, -1, NU, unit - 1)
                wait_item(act, heads_ok, at, -1, NU, unit - 1)
                ps = value_bank[u][:].rearrange("p (a g h n) -> p a g h n", a=UP, g=2, h=2)
                lg, inv = log_sum[:, unit % 2], inv_sum[:, unit % 2]
                flat = lambda x: x.rearrange("p a h n -> p a (h n)")
                nc.scalar.activation(flat(lg[0:64]), flat(ps[64:128, :, 0]), ACT.Ln)
                nc.scalar.activation(flat(lg[64:128]), flat(ps[0:64, :, 1]), ACT.Ln).then_inc(log_ok, 1)
                wait_item(act, log_ok, at, -1, NU, unit + 1)
                nc.scalar.activation(flat(inv), flat(lg), ACT.Exp, scale=-1.0).then_inc(inv_ok, 1)

            def tick(at, c):
                if live(at, -3) and c == 2:
                    wait_item(act, y_ps, at, -3, 1, 1)
                    slot = (at.j - 3) % 2
                    if at.known is None or at.known >= 5:
                        act.wait_ge(y_stored[slot], at.index(-3, 2) * 16)
                    nc.scalar.activation(width_modes[:, slot, :], out_bank[0:KW, :], ACT.Copy).then_inc(y_ok, 1)
                if live(at, -1, c):
                    wait_item(act, qk_ps, at, -1, NC, c + 1)
                    wait_item(act, ops2_ok, at, -1, NC, c - 1)
                    flat = lambda x: x.rearrange("p w n -> p (w n)")
                    nc.scalar.activation(flat(q_sb[:, c % 2]), qk_bank[:, 0:256], ACT.Identity, bias=b_q[:])
                    nc.scalar.activation(flat(k_sb[:, c % 2]), qk_bank[:, 256:512], ACT.Identity,
                                         bias=b_in[:, 1:2]).then_inc(qk_ok, 1)
                exponentials(at, c - 2, 0)
                if live(at, -1, c):
                    wait_item(act, v_ps, at, -1, NC, c + 1)
                    wait_item(act, vt_ps, at, -1, NC, c - 1)
                    src = mix_bank[:, 0:256].rearrange("p (w n) -> p w n", n=N)
                    nc.scalar.activation(v_diag[0:64, c % 2, :, 0:64], src[0:64], ACT.Identity, bias=b_in[0:64, 2:3])
                    nc.scalar.activation(v_diag[64:128, c % 2, :, 64:128], src[64:128], ACT.Identity,
                                         bias=b_in[64:128, 2:3]).then_inc(vd_ok, 1)
                inverse_sums(at, c - 3, 0)
                exponentials(at, c - 2, 1)
                inverse_sums(at, c - 3, 1)
                if live(at, -3) and 2 <= c < 6:
                    q = c - 2
                    wait_item(act, x1_ok, at, -3, NG, NG)
                    wait_item(act, sum_ok, at, -3, NG, q - 3)
                    nc.scalar.activation(sq[:, q, :], xs[:, (at.j - 3) % RING, 2 * q:2 * q + 2].rearrange("p r i a c -> p (r i a c)"),
                                         ACT.Square).then_inc(sq_ok, 1)

            def body(at):
                for c in range(NC):
                    tick(at, c)

            act.wait_ge(consts, 176)
            act.wait_ge(zeroed, ZEROED)
            nc.scalar.preload_act_table_set("natural_log_exp_and_others")
            with act.Fori(0, IMG) as img:
                act.wait_ge(img_set, (img + 1) * SET_STEPS)
                sweep(act, img, body)
                join(act, img)

        @block.vector
        def _(dve):
            def maximum(at, t, u):
                if not live(at, -1, t):
                    return
                unit = UN * t + u
                wait_item(dve, peak_ps, at, -1, NU, unit + 1)
                nc.vector.tensor_reduce(peak[:, unit % 2, :], peak_bank[:].rearrange("p (a n) -> p a n", n=N),
                                        axis=AX.X, op=ALU.max).then_inc(peak_ok, 1)
                wait_item(dve, peak_ok, at, -1, NU, unit + 1)
                wait_item(dve, score_ps, at, -1, NU, unit - 3)
                nc.vector.tensor_tensor(
                    peak_diag[:, unit % 4].rearrange("p a h n -> p (a h) n"),
                    token_eye[:].unsqueeze(1).to_broadcast([P, UP * NH, N]),
                    peak[:, unit % 2, :].unsqueeze(2).to_broadcast([P, UP * NH, N]), ALU.mult).then_inc(pd_ok, 1)

            def normalise(at, t, u):
                if not live(at, -1, t):
                    return
                unit = UN * t + u
                if t == 0 and u == 0:
                    wait_item(dve, out_ps, at, -3, NG, NG)
                wait_item(dve, inv_ok, at, -1, NU, unit + 1)
                ps = value_bank[u][:].rearrange("p (a g h n) -> p a g h n", a=UP, g=2, h=2)
                w = CH * (t % NC) + UP * u
                ring = (at.j - 1 if t >= 0 else at.j - 2) % 2
                for g in range(2):
                    rows = slice(64 * g, 64 * g + 64)
                    split = lambda x: x.rearrange("p a h (k j) -> p a h k j", j=4)
                    last = nc.vector.tensor_tensor(
                        heads[rows, ring, :, :, w:w + UP, :].rearrange("p h k a j -> p a h k j"), split(ps[rows, :, g]),
                        split(inv_sum[rows, unit % 2]), ALU.mult)
                last.then_inc(heads_ok, 1)

            def tick(at, c):
                maximum(at, c - 1, 0)
                normalise(at, c - 3, 0)
                if live(at, -1, c):
                    wait_item(dve, vt_ps, at, -1, NC, c + 1)
                    wait_item(dve, value_ps, at, -1, NU, UN * (c - 3))
                    src = out_bank[:].rearrange("p (w ab g k) -> p w ab g k", w=CH, ab=2, g=2)
                    for g in range(2):
                        dst = v_ones[:, c % 4, :, g, 64 * g:64 * g + 64].rearrange("p w (ab k) -> p w ab k", ab=2)
                        last = nc.vector.tensor_copy(dst, src[:, :, :, g, :])
                    last.then_inc(vo_ok, 1)
                maximum(at, c - 1, 1)
                normalise(at, c - 3, 1)
                if c % 2 and live(at, 0):
                    g = c // 2
                    wait_item(dve, xt_ps, at, 0, NG, g + 1)
                    dst = xt[:, at.j % 2].rearrange("p w (k j) -> p k w j", j=4)[:, GRP * g:GRP * (g + 1)]
                    add = mod_cur[:].rearrange("p (k j) -> p k j", j=4)[:, GRP * g:GRP * (g + 1), :]
                    nc.vector.tensor_tensor(dst, mix_bank[:].rearrange("p (k w j) -> p k w j", k=GRP, j=4),
                                            add.unsqueeze(2).to_broadcast([P, GRP, WP, 4]), ALU.add).then_inc(xt_ok, 1)
                if c >= 4 and live(at, -2):
                    g = c - 4
                    wait_item(dve, out_ps, at, -2, NG, g + 1)
                    row = xs[:, (at.j - 2) % RING, 2 * g:2 * g + 2].rearrange("p r i a c -> p (r i a c)")
                    nc.vector.tensor_tensor(row, out_bank[:], row, ALU.add).then_inc(x1_ok, 1)

            def body(at):
                for c in range(NC):
                    tick(at, c)

            nc.vector.memset(v_diag[:], 0.0).then_inc(zeroed, 1)
            nc.vector.memset(v_ones[:], 0.0).then_inc(zeroed, 1)
            nc.vector.memset(b_out[:].bitcast(F32), 0.0).then_inc(zeroed, 1)
            nc.vector.memset(ones_r[:].bitcast(F32), 1.0).then_inc(zeroed, 1)
            dve.wait_ge(zeroed, 4)
            for ab in range(2):
                for g in range(2):
                    o = 64 * (1 - g) + 32 * ab
                    nc.vector.memset(v_ones[64 * ab:64 * ab + 64, :, :, g, o:o + 32], 1.0).then_inc(zeroed, 1)
            dve.wait_ge(consts, 176)
            nc.vector.tensor_copy(neg_same_r[:], neg_same[:]).then_inc(zeroed, 1)
            nc.vector.tensor_scalar(b_q[:], b_in[:, 0:1], float(HD) ** -0.5, None, ALU.mult).then_inc(zeroed, 1)
            nc.vector.tensor_copy(b_out[0:1, :], b_rows[:, 0, :]).then_inc(zeroed, 1)
            dve.wait_ge(zeroed, 11)
            nc.vector.tensor_tensor(b_lo[:], b_rows[:, 0, :], b_out[0:1, :].bitcast(F32), ALU.subtract).then_inc(zeroed, 1)
            dve.wait_ge(zeroed, 12)
            nc.vector.tensor_copy(b_out[32:33, :], b_lo[:]).then_inc(zeroed, 1)

            with dve.Fori(0, IMG) as img:
                st = stats1[:, img, :]
                for i in range(3):
                    nc.vector.tensor_scalar(w_cur[:, i, :], w_in[:, i, :], st[:, 2:3],
                                            float(HD) ** -0.5 if i == 0 else 1.0, ALU.mult, ALU.mult).then_inc(img_set, 1)
                nc.vector.tensor_scalar(mod_cur[:], mod[:], st[:, 1:2], st[:, 0:1], ALU.mult, ALU.subtract)\
                    .then_inc(img_set, 1)
                nc.vector.memset(sum_sq[:], 0.0).then_inc(img_set, 1)
                dve.wait_ge(img_set, (img + 1) * SET_STEPS)
                sweep(dve, img, body)
                dve.wait_ge(sum_ps, img + 1)
                nc.vector.tensor_copy(sqsum[:, bass.ds(img, 1)], out_bank[:, 0:1]).then_inc(img_done, 1)
                join(dve, img)

        @block.gpsimd
        def _(pool):
            def tick(at, c):
                if live(at, -1, c):
                    q, k = q_sb[:, c % 2], k_sb[:, c % 2]
                    wait_item_apart(pool, peak_ps, at, -1, NU, UN * (c - 1), passed)
                    wait_item_apart(pool, qk_ok, at, -1, NC, c + 1, passed)
                    for h in range(NH):
                        nc.gpsimd.tensor_scalar(k_heads[:, c % 2, :, h, :], k, head_mask[:, h:h + 1], 1.0, ALU.mult, ALU.mult)
                    for ab in range(2):
                        last = nc.gpsimd.tensor_scalar(q_diag[:, c % 2, :, 64 * ab:64 * ab + 64], q,
                                                       half_mask[:, ab:ab + 1], 1.0, ALU.mult, ALU.mult)
                    last.then_inc(ops1_ok, 1)
                    wait_item_apart(pool, score_ps, at, -1, NU, UN * (c - 3), passed)
                    for h in range(NH):
                        nc.gpsimd.tensor_scalar(q_heads[:, c % 4, :, h, :], q, head_mask[:, h:h + 1], 1.0, ALU.mult, ALU.mult)
                    for ab in range(2):
                        last = nc.gpsimd.tensor_scalar(k_diag[:, c % 4, :, 64 * ab:64 * ab + 64], k,
                                                       half_mask[:, ab:ab + 1], 1.0, ALU.mult, ALU.mult)
                    last.then_inc(ops2_ok, 1)
                if live(at, -3) and 3 <= c < 7:
                    q = c - 3
                    wait_item(pool, sq_ok, at, -3, NG, q + 1)
                    wait_item(pool, sum_ok, at, -3, NG, q - 3)
                    nc.gpsimd.tensor_tensor(sum_sq[:, q, :], sum_sq[:, q, :], sq[:, q, :], ALU.add).then_inc(sum_ok, 1)

            def body(at):
                for c in range(NC):
                    tick(at, c)

            pool.wait_ge(consts, 176)
            pool.wait_ge(zeroed, ZEROED)
            with pool.Fori(0, IMG) as img:
                pool.wait_ge(img_set, (img + 1) * SET_STEPS)
                sweep(pool, img, body)
                join(pool, img)


ZEROED = 13
SET_STEPS = 5


def pass3(nc, ext, y1, sqsum, group_avg, back, IMG, H):
    HB = min(P, H)
    HQ = H // HB
    IC = 2 * IMG
    WR = 4
    NB = 8
    PARTS = [(n, min(n + NB, M2)) for n in range(0, M2, NB)]
    yv = y1.rearrange("i k (q p c) -> i q p k c", q=HQ, p=HB)
    with ExitStack() as c:
        sb = lambda n, shape, dt=F32: c.enter_context(nc.sbuf_tensor(n, shape, dt))
        yt = sb("yt", [HB, HQ, KW, C])
        fwd_h = sb("fwd_h", [HB, HQ, 2, 2 * M1])
        ident = sb("p3_ident", [P, P])
        mode_parts = sb("mode_parts", [2 * M1, P])
        group_mean2 = sb("group_mean2", [P, P])
        modes = sb("modes", [2 * M1, M2, C])
        dc = sb("dc", [P, 1])
        stats = sb("p3_stats", [P, 3])
        work = sb("p3_work", [P, 3])
        shift = sb("shift", [P, 1])
        ready = sb("p3_ready", [P, 2])
        mixed_in = sb("mixed_in", [P, M1, M2, IC])
        col = sb("col", [P, WR, M2, IC])
        wt = sb("wt", [P, WR, M2, C])
        mixed = sb("mixed", [C, IMG, M2, 2, M1])
        mixed_img = sb("mixed_img", [C, M2, 2 * M1])
        bank = lambda n: c.enter_context(nc.psum_tensor(n, [P, 512], F32))
        h_bank, t_bank, m_bank = [[bank(f"p3_{k}{i}") for i in range(2)] for k in ("h", "t", "m")]
        stat_bank = bank("p3_stat")
        sem = lambda n: c.enter_context(nc.semaphore(n))
        consts, cleared = sem("p3_consts"), sem("p3_cleared")
        y_ok = sem("p3_y_ok")
        h_ps, h_ok = sem("p3_h_ps"), sem("p3_h_ok")
        dc_ps, dc_ok, avg = sem("p3_dc_ps"), sem("p3_dc_ok"), sem("p3_avg")
        chain, dev, shift_ok = sem("p3_chain"), sem("p3_dev"), sem("p3_shift")
        t_ps, t_ok, fixed = sem("p3_t_ps"), sem("p3_t_ok"), sem("p3_fixed")
        w_ok = [sem(f"p3_w{i}") for i in range(WR)]
        col_ok, m_ps, m_ok = sem("p3_col_ok"), sem("p3_m_ps"), sem("p3_m_ok")
        i_ok, b_ps, b_ok = sem("p3_i_ok"), sem("p3_b_ps"), sem("p3_b_ok")
        passed = sem("p3_passed")
        NP_ = len(PARTS)
        wv = ext["w_mix"].rearrange("m p (n o) -> m p n o", n=M2)
        block = c.enter_context(nc.Block())

        @block.sync
        def _(sp):
            for dst, name in ((ident, "ident"), (mode_parts, "mode_parts"), (group_mean2, "group_mean2")):
                sp.dma_start(dst[:], ext[name]).then_inc(consts, 16)
            sp.dma_start(fwd_h[:].rearrange("p q a m -> p (q a m)"), ext["fwd_h"]).then_inc(consts, 16)
            for i in range(WR):
                sp.dma_start(wt[:, i], wv[i]).then_inc(w_ok[i], 16)
            for q in range(HQ):
                sp.dma_start(yt[:, q], yv[0, q]).then_inc(y_ok, 16)
            for img in range(1, IMG):
                sp.wait_ge(h_ps, img * NP_)
                for q in range(HQ):
                    sp.dma_start(yt[:, q], yv[img, q]).then_inc(y_ok, 16)
            with sp.Fori(1, M1 // WR) as quad:
                for i in range(WR):
                    sp.wait_ge(m_ps, quad * WR + (i - WR + 1))
                    sp.dma_start(wt[:, i], wv[quad * WR + i]).then_inc(w_ok[i], 16)

        @block.tensor
        def _(pe):
            pe.wait_ge(consts, 64)
            with pe.Fori(0, IMG) as img:
                pe.wait_ge(y_ok, (img + 1) * (16 * HQ))
                for k, (n0, n1) in enumerate(PARTS):
                    ps = h_bank[k % 2]
                    if k >= 2:
                        pe.wait_ge(h_ok, img * NP_ + (k - 1))
                    w = (n1 - n0) * C
                    for q in range(HQ):
                        for part in range(2):
                            last = nc.tensor.matmul(
                                ps[0:2 * M1, 0:w], fwd_h[:, q, part, :],
                                yt[:, q, part * M2 + n0:part * M2 + n1, :].rearrange("p n c -> p (n c)"),
                                start=(q == 0 and part == 0), stop=(q == HQ - 1 and part == 1))
                    last.then_inc(h_ps, 1)
                wait_apart(pe, h_ok, (img + 1) * NP_, passed)
                for half in range(2):
                    last = nc.tensor.matmul(stat_bank[64 * half:64 * half + 64, 4:5], modes[:, 0, :],
                                            ident[0:2 * M1, M1 // 2:M1 // 2 + 1], start=True, stop=True)
                last.then_inc(dc_ps, 1)
                pe.wait_ge(dc_ok, 2 * img + 2)
                nc.tensor.matmul(stat_bank[:, 0:1], group_mean2[:], dc[:], start=True, stop=True)
                nc.tensor.matmul(stat_bank[:, 1:2], group_avg[:], work[:, 2:3], start=True, stop=True).then_inc(avg, 1)
                for k, (n0, n1) in enumerate(PARTS):
                    if k >= 2:
                        wait_apart(pe, t_ok, img * NP_ + (k - 1), passed)
                    for n in range(n0, n1):
                        for half in range(2):
                            last = nc.tensor.matmul(
                                t_bank[k % 2][64 * half:64 * half + 64, (n - n0) * 64:(n - n0 + 1) * 64],
                                modes[:, n, :], mode_parts[:, 64 * half:64 * half + 64], start=True, stop=True)
                    last.then_inc(t_ps, 1)
                pe.wait_ge(fixed, 2 * img + 2)
            with pe.Fori(0, M1 // WR) as quad:
                for i in range(WR):
                    pe.wait_ge(w_ok[i], (quad + 1) * 16)
                    pe.wait_ge(col_ok, quad * WR + (i + 1))
                    pe.wait_ge(m_ok, quad * WR + (i + 1))
                    for n in range(M2):
                        last = nc.tensor.matmul(m_bank[i % 2][0:C, n * IC:(n + 1) * IC], wt[:, i, n, :],
                                                col[:, i, n, :], start=True, stop=True)
                    last.then_inc(m_ps, 1)
            with pe.Fori(0, IMG) as img:
                pe.wait_ge(i_ok, img + 1)
                for k, (n0, n1) in enumerate(PARTS):
                    wait_apart(pe, b_ok, img * NP_ + (k + 1), passed)
                    for n in range(n0, n1):
                        for half in range(2):
                            last = nc.tensor.matmul(
                                h_bank[k % 2][64 * half:64 * half + 64, (n - n0) * C:(n - n0 + 1) * C],
                                mixed_img[:, n, :], ident[0:C, 0:C], start=True, stop=True)
                    last.then_inc(b_ps, 1)

        @block.scalar
        def _(act):
            with act.Fori(0, IMG) as img:
                for k, (n0, n1) in enumerate(PARTS):
                    act.wait_ge(h_ps, img * NP_ + (k + 1))
                    nc.scalar.activation(modes[:, n0:n1, :].rearrange("p n c -> p (n c)"),
                                         h_bank[k % 2][0:2 * M1, 0:(n1 - n0) * C], ACT.Copy).then_inc(h_ok, 1)
                act.wait_ge(chain, img * 4 + 3)
                nc.scalar.activation(stats[:, 1:2], work[:, 2:3], ACT.Sqrt).then_inc(dev, 1)
                act.wait_ge(fixed, img * 2 + 2)
            with act.Fori(0, M1 // WR) as quad:
                for i in range(WR):
                    act.wait_ge(m_ps, quad * WR + (i + 1))
                    nc.scalar.activation(mixed[:, :, :, :, quad * WR + i].rearrange("p i n r -> p n r i"),
                                         m_bank[i % 2][0:C, 0:M2 * IC].rearrange("p (n r i) -> p n r i", n=M2, r=2),
                                         ACT.Copy).then_inc(m_ok, 1)

        @block.vector
        def _(dve):
            nc.vector.memset(back[:], 0.0).then_inc(cleared, 1)
            nc.vector.memset(ready[:, 0:1], 0.0).then_inc(m_ok, 2)
            nc.vector.memset(ready[:, 1:2], 0.0).then_inc(b_ok, 2)
            with dve.Fori(0, IMG) as img:
                dve.wait_ge(dc_ps, img + 1)
                nc.vector.tensor_copy(dc[:], stat_bank[:, 4:5]).then_inc(dc_ok, 1)
                nc.vector.tensor_copy(work[:, 2:3], sqsum[:, bass.ds(img, 1)]).then_inc(dc_ok, 1)
                dve.wait_ge(avg, img + 1)
                group_stats(nc, dve, stats, stat_bank, work, chain, img * 4, dev, img)
                nc.vector.tensor_tensor(shift[:], stats[:, 0:1], stats[:, 2:3], ALU.mult).then_inc(shift_ok, 1)
                for k, (n0, n1) in enumerate(PARTS):
                    dve.wait_ge(t_ps, img * NP_ + (k + 1))
                    src = t_bank[k % 2][:, 0:(n1 - n0) * 64].rearrange("p (n r m) -> p n r m", r=2, m=M1)
                    cols = mixed_in[:, :, n0:n1, :].rearrange("p m n (r i) -> p n r m i", r=2)
                    nc.vector.tensor_scalar(cols[:, :, :, :, img], src, stats[:, 2:3], None, ALU.mult).then_inc(t_ok, 1)
                dve.wait_ge(t_ok, (img + 1) * NP_)
                dve.wait_ge(shift_ok, img + 1)
                for half in range(2):
                    rows = slice(64 * half, 64 * half + 64)
                    at = mixed_in[rows, M1 // 2, 0:1, :].rearrange("p n (r i) -> p n r i", r=2)[:, :, half, img]
                    nc.vector.tensor_scalar(at, at, shift[rows, :], None, ALU.subtract).then_inc(fixed, 1)
                dve.wait_ge(fixed, img * 2 + 2)
            with dve.Fori(0, M1 // WR) as quad:
                for i in range(WR):
                    dve.wait_ge(m_ok, quad * WR + (i + 1))
                    nc.vector.tensor_copy(col[:, i].rearrange("p n i -> p (n i)"),
                                          mixed_in[:, quad * WR + i].rearrange("p n i -> p (n i)")).then_inc(col_ok, 1)
            dve.wait_ge(m_ok, M1 + 2)
            dve.wait_ge(cleared, 1)
            with dve.Fori(0, IMG) as img:
                nc.vector.tensor_copy(mixed_img[:].rearrange("p n m -> p (n m)"),
                                      mixed[:, img].rearrange("p n r m -> p (n r m)")).then_inc(i_ok, 1)
                for k, (n0, n1) in enumerate(PARTS):
                    dve.wait_ge(b_ps, img * NP_ + (k + 1))
                    for half in range(2):
                        rows = slice(64 * half, 64 * half + 64)
                        last = nc.vector.tensor_copy(
                            back[rows, img, :, half * M2 + n0:half * M2 + n1].rearrange("p c n -> p n c"),
                            h_bank[k % 2][rows, 0:(n1 - n0) * C].rearrange("p (n c) -> p n c", c=C))
                    last.then_inc(b_ok, 1)


def pass4(nc, ext, x1, back, out, IMG, H):
    HB = min(P, H)
    HQ = H // HB
    SB = HB // PS
    CG = 512 // HB
    GC = C // CG
    TB = 4
    xv = x1.rearrange("(g r) (p e) -> g p r e", r=PS, p=P)
    ov = out.rearrange("(g r) (p e) -> g p r e", r=PS, p=P)
    with ExitStack() as c:
        sb = lambda n, shape: c.enter_context(nc.sbuf_tensor(n, shape, F32))
        inv_h = sb("inv_h", [P, H])
        inv_w = sb("inv_w", [KW, 4, P])
        lines = sb("lines", [KW, HB, C])
        now = sb("now", [P, C, KW])
        tile = sb("p4_x", [P, TB, PS, 4, C])
        ready = sb("p4_ready", [P, 2])
        bank = lambda n: c.enter_context(nc.psum_tensor(n, [P, 512], F32))
        l_bank = [bank(f"p4_l{i}") for i in range(2)]
        y_bank = [bank(f"p4_y{i}") for i in range(4)]
        sem = lambda n: c.enter_context(nc.semaphore(n))
        consts, now_ok = sem("p4_consts"), sem("p4_now_ok")
        loaded = [sem(f"p4_loaded{i}") for i in range(TB)]
        stored = [sem(f"p4_stored{i}") for i in range(TB)]
        l_ps, l_ok = sem("p4_l_ps"), sem("p4_l_ok")
        y_ps, y_ok = sem("p4_y_ps"), sem("p4_y_ok")
        passed = sem("p4_passed")
        block = c.enter_context(nc.Block())
        STRIPS = IMG * H // PS

        @block.sync
        def _(sp):
            sp.dma_start(inv_h[:], ext["inv_h"]).then_inc(consts, 16)
            sp.dma_start(inv_w[:].rearrange("k i p -> k (i p)"), ext["inv_w"]).then_inc(consts, 16)
            for t in range(TB):
                sp.dma_start(tile[:, t].rearrange("p r i c -> p r (i c)"), xv[t]).then_inc(loaded[t], 16)
            with sp.Fori(0, STRIPS // TB - 1) as i:
                for t in range(TB):
                    sp.wait_ge(y_ok, (i * TB + (t + 2)) * 4)
                    sp.dma_start(ov[i * TB + t], tile[:, t].rearrange("p r i c -> p r (i c)")).then_inc(stored[t], 16)
                    if t:
                        sp.wait_ge(stored[t - 1], (i + 1) * 16)
                        sp.dma_start(tile[:, t - 1].rearrange("p r i c -> p r (i c)"), xv[i * TB + (TB + t - 1)])\
                            .then_inc(loaded[t - 1], 16)
                sp.wait_ge(stored[TB - 1], (i + 1) * 16)
                sp.dma_start(tile[:, TB - 1].rearrange("p r i c -> p r (i c)"), xv[i * TB + (2 * TB - 1)])\
                    .then_inc(loaded[TB - 1], 16)
            for t in range(TB):
                sp.wait_ge(y_ok, (STRIPS - TB + t + 2) * 4)
                sp.dma_start(ov[STRIPS - TB + t], tile[:, t].rearrange("p r i c -> p r (i c)")).then_inc(stored[t], 16)
            for t in range(TB):
                sp.wait_ge(stored[t], (STRIPS // TB) * 16)

        @block.tensor
        def _(pe):
            pe.wait_ge(consts, 32)
            with pe.Fori(0, IMG) as img:
                wait_apart(pe, now_ok, img + 1, passed)
                with pe.Fori(0, HQ) as hq:
                    blk = img * HQ + hq
                    for g in range(GC):
                        wait_apart(pe, l_ok, blk * GC + (g + 1), passed)
                        for i in range(CG):
                            last = nc.tensor.matmul(l_bank[g % 2][0:KW, i * HB:(i + 1) * HB], now[:, g * CG + i, :],
                                                    inv_h[:, bass.ds(hq * HB, HB)], start=True, stop=True)
                        last.then_inc(l_ps, 1)
                    wait_apart(pe, l_ok, blk * GC + (GC + 2), passed)
                    with pe.Fori(0, SB // 2) as s:
                        for t in range(2):
                            for i in range(4):
                                q = 4 * t + i
                                wait_apart(pe, y_ok, (blk * SB + s * 2) * 4 + (q + 1), passed)
                                nc.tensor.matmul(y_bank[q % 4][:], inv_w[:, i, :],
                                                 lines[:, bass.ds(s * (2 * PS) + t * PS, PS), :].rearrange("k r c -> k (r c)"),
                                                 start=True, stop=True).then_inc(y_ps, 1)

        @block.scalar
        def _(act):
            with act.Fori(0, IMG * HQ) as blk:
                for g in range(GC):
                    act.wait_ge(l_ps, blk * GC + (g + 1))
                    if g == 0:
                        act.wait_ge(y_ok, blk * (4 * SB) + 4)
                    nc.scalar.activation(lines[:, :, g * CG:(g + 1) * CG].rearrange("k h c -> k c h"),
                                         l_bank[g % 2][0:KW, :].rearrange("k (c h) -> k c h", c=CG), ACT.Copy)\
                        .then_inc(l_ok, 1)

        @block.vector
        def _(dve):
            nc.vector.memset(ready[:, 0:1], 0.0).then_inc(l_ok, 2)
            nc.vector.memset(ready[:, 1:2], 0.0).then_inc(y_ok, 4)
            with dve.Fori(0, IMG) as img:
                dve.wait_ge(l_ok, img * (HQ * GC) + 2)
                nc.vector.tensor_copy(now[:].rearrange("p c k -> p (c k)"),
                                      back[:, img].rearrange("p c k -> p (c k)")).then_inc(now_ok, 1)
                with dve.Fori(0, HQ * SB // TB) as s:
                    for t in range(TB):
                        strips = img * (HQ * SB) + (s * TB + t)
                        dve.wait_ge(loaded[t], (img * (HQ * SB // TB) + (s + 1)) * 16)
                        for i in range(4):
                            dve.wait_ge(y_ps, strips * 4 + (i + 1))
                            at = tile[:, t, :, i, :]
                            nc.vector.tensor_tensor(at, y_bank[i][:].rearrange("p (r c) -> p r c", c=C), at, ALU.add)\
                                .then_inc(y_ok, 1)


def block_diagonal(a, b):
    m = np.zeros((a.shape[0] + b.shape[0], a.shape[1] + b.shape[1]), a.dtype)
    m[:a.shape[0], :a.shape[1]] = a
    m[a.shape[0]:, a.shape[1]:] = b
    return m


def layout(x, modulator, w_qkv, b_qkv, w_proj, b_proj, w_real, w_imag):
    a = {"x": x.reshape(-1, W * C)}
    parts = [w_qkv[i * C:(i + 1) * C].T for i in range(3)]
    a["w_in"] = np.stack([block_diagonal(w, w) for w in parts], 1)
    a["b_in"] = np.stack([np.concatenate([b, b]) for b in b_qkv.reshape(3, C)], 1)
    m = modulator.reshape(PS, 4, 2, C).transpose(3, 0, 2, 1).reshape(C, N)
    a["mod"] = np.concatenate([m, m])
    w = w_proj.T.reshape(2, 2, HD, C)
    o = np.zeros((2, 2, 2, HD, 2, 2, C), w_proj.dtype)
    for ab in range(2):
        for h in range(2):
            o[:, ab, h, :, h, ab, :] = w[:, h]
    a["w_out"] = o.reshape(P, 2, P)
    a["b_out"] = np.tile(b_proj, 16).reshape(1, 2, 512)
    a["w_mix"] = np.stack([w_real, w_imag], 1).transpose(0, 1, 3, 2, 4).reshape(M1, P, M2 * C)
    return {k: np.ascontiguousarray(v) for k, v in a.items()}


_OUT = ((4, 512, 512, 64), "float32")


def kernel(**inputs):
    import concourse.bacc as _bacc
    from concourse.bass_utils import run_bass_kernel_spmd as _run

    f = {k: np.asarray(v) for k, v in inputs.items()}
    x = f["x"]
    arrays = layout(x, f["L0_conv_modulator"], f["L0_conv_w_qkv"], f["L0_conv_b_qkv"], f["L0_conv_w_proj"],
                    f["L0_conv_b_proj"], f["L1_conv_W_real"], f["L1_conv_W_imag"])
    arrays.update(tables(x.shape[1]))
    nc = _bacc.Bacc("TRN2", target_bir_lowering=False, num_devices=1)
    ext = {k: nc.dram_tensor(f"in_{k}", v.shape, mybir.dt.from_np(v.dtype), kind="ExternalInput").ap()
           for k, v in arrays.items()}
    out = nc.dram_tensor("out", (x.shape[0] * x.shape[1], W * C), F32, kind="ExternalOutput").ap()
    program(nc, ext, out, x.shape[0], x.shape[1])
    r = _run(nc, [{f"in_{k}": v for k, v in arrays.items()}], core_ids=[0])
    return r.results[0]["out"].reshape(x.shape)
```

```python
from contextlib import ExitStack

import numpy as np

import concourse.bass as bass
from concourse import mybir

F32 = mybir.dt.float32
F32R = mybir.dt.float32r
ACT = mybir.ActivationFunctionType
ALU = mybir.AluOpType
AX = mybir.AxisListType

C = 64
W = 512
P = 128
NH = 4
HD = C // NH
PS = 8
N = PS * PS
M1, M2 = 32, 17
KW = 2 * M2
E = 2 * C
WP = W // (2 * PS)
CH = 4
NC = WP // CH
ROW = PS * 2 * E
GRP = 4
NG = 2 * PS // GRP
RING = 4
EPS = 1e-5


def tables(H):
    p = np.arange(P)
    t = {}
    wpix = (256 * np.arange(2)[:, None] + np.arange(2)[None, :])[None] + 2 * p[:, None, None]
    ang = 2 * np.pi * ((wpix[..., None] * np.arange(M2)) % W) / W
    t["fwd_w"] = (np.concatenate([np.cos(ang), -np.sin(ang)], -1) / W).reshape(P, 4 * KW)
    kh = np.arange(M1) - M1 // 2
    h = np.arange(H)
    ang = 2 * np.pi * ((h[:, None] * kh) % H) / H
    c, s = np.cos(ang) / H, np.sin(ang) / H
    fwd_h = np.stack([np.concatenate([c, -s], 1), np.concatenate([s, c], 1)], 1)
    hp = min(P, H)
    t["fwd_h"] = fwd_h.reshape(H // hp, hp, 2, 2 * M1).transpose(1, 0, 2, 3).reshape(hp, -1)
    c, s = np.cos(ang).T, np.sin(ang).T
    t["inv_h"] = np.concatenate([c, -s, s, c], 0)
    a = np.where(np.arange(M2) == 0, 1.0, 2.0)[:, None]
    wpix = (4 * p[None, :] + np.arange(4)[:, None]).reshape(-1)
    ang = 2 * np.pi * ((np.arange(M2)[:, None] * wpix) % W) / W
    t["inv_w"] = np.concatenate([a * np.cos(ang), -a * np.sin(ang)], 0)
    t["ident"] = np.eye(P)
    t["token_eye"] = np.concatenate([np.eye(N), np.eye(N)], 0)
    t["head_mask"] = ((p[:, None] % C) // HD == np.arange(NH)).astype(float)
    t["half_mask"] = (p[:, None] // C == np.arange(2)).astype(float)
    t["other_head"] = np.where((p[:, None] // HD) % 2 == np.arange(2), 0.0, -1000.0)
    same = (p[:, None] // C) == (p[None, :] // C)
    t["neg_same_window"] = -same.astype(float)
    t["group_avg"] = (((p[:, None] % C) // 2) == ((p[None, :] % C) // 2)) / (2.0 * H * W)
    t["group_mean2"] = (same & ((p[:, None] // 2) == (p[None, :] // 2))) / 2.0
    z, i = np.zeros((M1, M1)), np.eye(M1)
    t["mode_parts"] = np.concatenate([np.eye(2 * M1), np.block([[z, i], [-i, z]])], 1)
    return {k: np.ascontiguousarray(v, np.float32) for k, v in t.items()}


class Place:

    def __init__(self, strips, img, quad, j, known=None):
        self.strips, self.img, self.quad, self.j, self.known = strips, img, quad, j, known

    def index(self, off=0, per=1):
        return self.img * (self.strips // per) + self.quad * (RING // per) + (self.j + off) // per

    def strip(self, off=0):
        return self.quad * RING + (self.j + off)


def wait_item(eng, sem, at, off, per, n):
    if at.known is None or per * (at.known + off) + n > 0:
        eng.wait_ge(sem, at.index(off) * per + n)


def wait_apart(eng, sem, value, passed):
    eng.wait_ge(sem, value).then_inc(passed, 1)


def wait_item_apart(eng, sem, at, off, per, n, passed):
    if at.known is None or per * (at.known + off) + n > 0:
        wait_apart(eng, sem, at.index(off) * per + n, passed)


def program(nc, ext, out, IMG, H):
    S = H // PS
    ctx = ExitStack()
    with ctx:
        def sb(stack, name, shape, dt=F32):
            return stack.enter_context(nc.sbuf_tensor(name, shape, dt))

        x1 = nc.dram_tensor("x1", [IMG * H, W * C], F32, kind="Internal").ap()
        y1 = nc.dram_tensor("y1", [IMG, KW, H * C], F32, kind="Internal").ap()

        stats1 = sb(ctx, "stats1", [P, IMG, 3])
        sqsum = sb(ctx, "sqsum", [P, IMG])
        ones = sb(ctx, "ones", [P, 1])
        group_avg = sb(ctx, "group_avg", [P, P])
        pass1(nc, ext, stats1, ones, group_avg, IMG, S)
        pass2(nc, ext, x1, y1, stats1, sqsum, ones, IMG, S)
        with ExitStack() as late:
            back = sb(late, "back", [P, IMG, C, KW])
            pass3(nc, ext, y1, sqsum, group_avg, back, IMG, H)
            pass4(nc, ext, x1, back, out, IMG, H)


def pass1(nc, ext, stats1, ones, group_avg, IMG, S):
    TB = 4
    PE_PARTS = 3
    Q = ROW // 4
    xt = ext["x"].rearrange("(t r) e -> t (r e)", r=PS).rearrange("t (p f) -> t p f", p=P)
    with ExitStack() as c:
        sb = lambda n, shape: c.enter_context(nc.sbuf_tensor(n, shape, F32))
        tile = sb("p1_x", [P, TB, ROW])
        sq = sb("p1_sq", [P, 2, ROW])
        sum_sq = sb("p1_sum_sq", [P, ROW])
        sum_x = sb("p1_sum_x", [P, Q])
        zero = sb("p1_zero", [P, Q])
        row = sb("p1_row", [1, Q])
        part = sb("p1_part", [P, 2])
        work = sb("p1_work", [P, 3])
        row_ps = c.enter_context(nc.psum_tensor("p1_row_ps", [P, Q], F32))
        part_ps = c.enter_context(nc.psum_tensor("p1_part_ps", [P, Q], F32))
        avg_ps = c.enter_context(nc.psum_tensor("p1_avg_ps", [P, Q], F32))
        sem = lambda n: c.enter_context(nc.semaphore(n))
        loaded = [sem(f"p1_loaded{i}") for i in range(TB)]
        consts, set_up, zeroed = sem("p1_consts"), sem("p1_set_up"), sem("p1_zeroed")
        pe_summed = sem("p1_pe_summed")
        sq_done = sem("p1_sq_done")
        sq_free = sem("p1_sq_free")
        x_summed = sem("p1_x_summed")
        pe_row, row_out = sem("p1_pe_row"), sem("p1_row_out")
        parts, parts_out, avg = sem("p1_parts"), sem("p1_parts_out"), sem("p1_avg")
        chain, dev = sem("p1_chain"), sem("p1_dev")
        passed = sem("p1_passed")
        CHAIN = 4
        block = c.enter_context(nc.Block())

        @block.sync
        def _(sp):
            sp.dma_start(group_avg[:], ext["group_avg"]).then_inc(consts, 16)
            for t in range(TB):
                sp.dma_start(tile[:, t, :], xt[t]).then_inc(loaded[t], 16)
            with sp.Fori(0, IMG * S // TB - 1) as i:
                for t in range(TB):
                    wait_apart(sp, pe_summed, i * TB + (t + 1), passed)
                    wait_apart(sp, sq_done, i * TB + (t + 1), passed)
                    sp.wait_ge(x_summed, i * TB + (t + 2))
                    sp.dma_start(tile[:, t, :], xt[i * TB + (TB + t)]).then_inc(loaded[t], 16)

        @block.tensor
        def _(pe):
            pe.wait_ge(set_up, 2)
            pe.wait_ge(consts, 16)
            for img in range(IMG):
                nc.tensor.matmul(row_ps[0:1, :], ones[:], zero[:], start=True, stop=False)
                with pe.Fori(0, S // TB) as i:
                    for t in range(TB):
                        pe.wait_ge(loaded[t], (i + (img * (S // TB) + 1)) * 16)
                        for q in range(PE_PARTS):
                            last = nc.tensor.matmul(row_ps[0:1, :], ones[:], tile[:, t, q * Q:(q + 1) * Q],
                                                    start=False, stop=False)
                        last.then_inc(pe_summed, 1)
                nc.tensor.matmul(row_ps[0:1, :], ones[:], zero[:], start=False, stop=True).then_inc(pe_row, 1)
                pe.wait_ge(row_out, img + 1)
                pe.wait_ge(x_summed, (img + 1) * S + 1)
                pe.wait_ge(sq_free, (img + 1) * S + 2)
                for k in range(Q // P):
                    nc.tensor.matmul(part_ps[:, 0:1], row[0:1, k * P:(k + 1) * P], ones[0:1, :],
                                     start=(k == 0), stop=False)
                for k in range(Q // P):
                    nc.tensor.matmul(part_ps[:, 0:1], sum_x[:, k * P:(k + 1) * P], ones[:],
                                     start=False, stop=(k == Q // P - 1))
                for k in range(ROW // P):
                    last = nc.tensor.matmul(part_ps[:, 1:2], sum_sq[:, k * P:(k + 1) * P], ones[:],
                                            start=(k == 0), stop=(k == ROW // P - 1))
                last.then_inc(parts, 1)
                pe.wait_ge(parts_out, img + 1)
                nc.tensor.matmul(avg_ps[:, 0:2], group_avg[:], part[:], start=True, stop=True).then_inc(avg, 1)

        @block.scalar
        def _(act):
            for img in range(IMG):
                with act.Fori(0, S // TB) as i:
                    for t in range(TB):
                        act.wait_ge(loaded[t], (i + (img * (S // TB) + 1)) * 16)
                        act.wait_ge(sq_free, i * TB + (img * S + t + 1))
                        nc.scalar.activation(sq[:, t % 2, :], tile[:, t, :], ACT.Square).then_inc(sq_done, 1)
                act.wait_ge(pe_row, img + 1)
                nc.scalar.activation(row[:], row_ps[0:1, :], ACT.Copy).then_inc(row_out, 1)
                act.wait_ge(chain, CHAIN * img + CHAIN - 1)
                nc.scalar.activation(stats1[:, img, 1:2], work[:, 2:3], ACT.Sqrt).then_inc(dev, 1)

        @block.vector
        def _(dve):
            nc.vector.memset(ones[:], 1.0).then_inc(set_up, 1)
            nc.vector.memset(zero[:], 0.0).then_inc(set_up, 1)
            nc.vector.memset(sq[:], 0.0).then_inc(sq_free, 2)
            nc.vector.memset(part[:], 0.0).then_inc(x_summed, 1)
            for img in range(IMG):
                nc.vector.memset(sum_sq[:], 0.0).then_inc(zeroed, 1)
                nc.vector.memset(sum_x[:], 0.0).then_inc(zeroed, 1)
                dve.wait_ge(zeroed, 2 * (img + 1))
                with dve.Fori(0, S // TB) as i:
                    for t in range(TB):
                        n = img * S + t
                        dve.wait_ge(sq_done, i * TB + (n + 1))
                        dve.wait_ge(sq_free, i * TB + (n + 2))
                        nc.vector.tensor_tensor(sum_sq[:], sum_sq[:], sq[:, t % 2, :], ALU.add).then_inc(sq_free, 1)
                        dve.wait_ge(x_summed, i * TB + (n + 1))
                        nc.vector.tensor_tensor(sum_x[:], sum_x[:], tile[:, t, PE_PARTS * Q:], ALU.add)\
                            .then_inc(x_summed, 1)
                dve.wait_ge(parts, img + 1)
                nc.vector.tensor_copy(part[:], part_ps[:, 0:2]).then_inc(parts_out, 1)
                dve.wait_ge(avg, img + 1)
                group_stats(nc, dve, stats1[:, img, :], avg_ps, work, chain, CHAIN * img, dev, img)


def group_stats(nc, dve, stats, avg_ps, work, chain, steps, dev, devs):
    nc.vector.tensor_copy(stats[:, 0:1], avg_ps[:, 0:1]).then_inc(chain, 1)
    dve.wait_ge(chain, steps + 1)
    nc.vector.tensor_tensor(work[:, 0:1], avg_ps[:, 0:1], stats[:, 0:1], ALU.mult).then_inc(chain, 1)
    dve.wait_ge(chain, steps + 2)
    nc.vector.tensor_tensor(work[:, 1:2], avg_ps[:, 1:2], work[:, 0:1], ALU.subtract).then_inc(dev, 1)
    dve.wait_ge(dev, 2 * devs + 1)
    nc.vector.tensor_scalar(work[:, 2:3], work[:, 1:2], 0.0, EPS, ALU.max, ALU.add).then_inc(chain, 1)
    dve.wait_ge(dev, 2 * devs + 2)
    nc.vector.reciprocal(stats[:, 2:3], stats[:, 1:2]).then_inc(chain, 1)
    dve.wait_ge(chain, steps + 4)


def pass2(nc, ext, x1, y1, stats1, sqsum, ones, IMG, S):
    UP = 2
    UN = CH // UP
    NU = NC * UN
    LO = 64
    strips = lambda a: a.rearrange("(g r) (ab p i c) -> g ab p r i c", r=PS, ab=2, p=P, i=2)
    xv, x1v = strips(ext["x"]), strips(x1)
    PARTS = [(i2, ab) for i2 in range(2) for ab in range(2)]
    y1v = y1.rearrange("i k (s e) -> i s k e", e=PS * C)
    with ExitStack() as c:
        sb = lambda n, shape, dt=F32: c.enter_context(nc.sbuf_tensor(n, shape, dt))
        xs = sb("xs", [P, RING, PS, 2, 2, C])
        xt = sb("xt", [P, WP, GRP, 4])
        xt_hi = sb("xt_hi", [P, 2, WP, N], F32R)
        xt_lo = sb("xt_lo", [P, 2, WP, N], F32R)
        q_sb = sb("q_sb", [P, 2, CH, N])
        k_sb = sb("k_sb", [P, 2, CH, N])
        k_heads = sb("k_heads", [P, 2, CH, NH, N], F32R)
        q_diag = sb("q_diag", [P, 2, CH, P], F32R)
        q_heads = sb("q_heads", [P, 4, CH, NH, N])
        k_diag = sb("k_diag", [P, 4, CH, P])
        v_diag = sb("v_diag", [P, 2, CH, P])
        v_ones = sb("v_ones", [P, 4, CH, 2, P])
        peak = sb("peak", [P, 2, UP * NH])
        peak_diag = sb("peak_diag", [P, 4, UP, NH, N], F32R)
        probs = sb("probs", [P, 4, UP, NH, N])
        log_sum = sb("log_sum", [P, 2, UP, 2, N])
        inv_sum = sb("inv_sum", [P, 2, UP, 2, N])
        weighted = sb("weighted", [P, 2, UP, 2, N])
        heads = sb("heads", [P, 2, 2 * PS, WP, 4])
        sq = sb("sq", [P, 2, ROW // NG])
        sum_sq = sb("sum_sq", [P, ROW // NG])
        x1_hi = sb("x1_hi", [P, PS, 2, 2, C], F32R)
        x1_lo = sb("x1_lo", [P, PS, 2, 2, C], F32R)
        width_modes = sb("width_modes", [KW, 2, PS * C])
        w_in = sb("w_in", [P, 3, P])
        b_in = sb("b_in", [P, 3])
        w_cur = sb("w_cur", [P, 3, P])
        w_hi = sb("w_hi", [P, 3, P], F32R)
        w_lo = sb("w_lo", [P, 3, P], F32R)
        b_q = sb("b_q", [P, 1])
        mod = sb("mod", [P, N])
        mod_cur = sb("mod_cur", [P, N])
        w_out = sb("w_out", [P, P])
        fwd_w = sb("fwd_w", [P, 4, KW])
        fwd_parts = sb("fwd_parts", [P, 4, LO + KW], F32R)
        ident = sb("ident", [P, P])
        token_eye = sb("token_eye", [P, N])
        head_mask = sb("head_mask", [P, NH])
        half_mask = sb("half_mask", [P, 2])
        other_head = sb("other_head", [P, 2])
        neg_same = sb("neg_same", [P, P])
        neg_same_r = sb("neg_same_r", [P, P], F32R)
        bank = lambda n: c.enter_context(nc.psum_tensor(n, [P, 512], F32))
        qk_bank, mix_bank, out_bank, peak_bank = bank("qk_bank"), bank("mix_bank"), bank("out_bank"), bank("peak_bank")
        score_bank = [bank(f"score_bank{i}") for i in range(2)]
        value_bank = [bank(f"value_bank{i}") for i in range(2)]
        sem = lambda n: c.enter_context(nc.semaphore(n))
        consts, zeroed, img_set = sem("consts"), sem("zeroed"), sem("img_set")
        loaded = [sem(f"loaded{i}") for i in range(RING)]
        stored = [sem(f"stored{i}") for i in range(RING)]
        y_stored = [sem(f"y_stored{i}") for i in range(2)]
        xt_ps, xt_sum, xt_ok = sem("xt_ps"), sem("xt_sum"), sem("xt_ok")
        xt_part = sem("xt_part")
        qk_ps, qk_ok = sem("qk_ps"), sem("qk_ok")
        v_ps, vd_ok = sem("v_ps"), sem("vd_ok")
        vt_ps, vo_ok = sem("vt_ps"), sem("vo_ok")
        ops1_ok, ops2_ok = sem("ops1_ok"), sem("ops2_ok")
        qd_ok = sem("qd_ok")
        peak_ps, peak_ok, pd_ok = sem("peak_ps"), sem("peak_ok"), sem("pd_ok")
        score_ps, probs_ok = sem("score_ps"), sem("probs_ok")
        value_ps, log_ok, inv_ok = sem("value_ps"), sem("log_ok"), sem("inv_ok")
        weighted_ok, heads_ok = sem("weighted_ok"), sem("heads_ok")
        out_ps, x1_ok = sem("out_ps"), sem("x1_ok")
        x_hi, x_lo = sem("x_hi"), sem("x_lo")
        y_ps, y_part, y_ok = sem("y_ps"), sem("y_part"), sem("y_ok")
        sq_ok, sum_ok = sem("sq_ok"), sem("sum_ok")
        sum_ps, img_done = sem("sum_ps"), sem("img_done")
        passed = sem("passed")
        joined = sem("joined")
        block = c.enter_context(nc.Block())

        def live(at, off, n=0, per=NC):
            return at.known is None or 0 <= per * (at.known + off) + n < per * S

        def sweep(eng, img, body, straight=0):
            for s in range(RING):
                body(Place(S, img, 0, s, known=s))
            if S // RING - straight // RING > 1:
                with eng.Fori(1, (S - straight) // RING) as quad:
                    for j in range(RING):
                        body(Place(S, img, quad, j))
            for s in range(max(S - straight, RING), S + 3):
                body(Place(S, img, s // RING, s % RING, known=s))

        def join(eng, img, x_stores=False, y_stores=False):
            wait_apart(eng, img_done, img + 1, joined)
            if x_stores:
                for i in range(RING):
                    wait_apart(eng, stored[i], (img + 1) * (64 * (S // RING)), joined)
            if y_stores:
                for i in range(2):
                    wait_apart(eng, y_stored[i], (img + 1) * (16 * (S // 2)), joined)

        @block.sync
        def _(sp):
            for dst, name in ((w_in, "w_in"), (b_in, "b_in"), (mod, "mod"), (w_out, "w_out"),
                              (fwd_w, "fwd_w"), (ident, "ident"), (token_eye, "token_eye"),
                              (head_mask, "head_mask"), (half_mask, "half_mask"), (other_head, "other_head"),
                              (neg_same, "neg_same_window")):
                sp.dma_start(dst[:], ext[name]).then_inc(consts, 16)

            def load(strip, slot):
                for i2, ab in PARTS:
                    sp.dma_start(xs[:, slot, :, i2, ab, :], xv[strip, ab, :, :, i2, :]).then_inc(loaded[slot], 16)

            def body(at, more):
                if live(at, 1) or (more and at.known == S - 1):
                    slot = (at.j + 1) % RING
                    if at.known is None or at.known >= RING - 1:
                        wait_item(sp, x_lo, at, -3, NG, NG)
                        wait_item(sp, sq_ok, at, -3, NG, NG)
                        sp.wait_ge(stored[slot], (at.index(-3, RING) + 1) * 64)
                    load(at.index(1), slot)
                if live(at, -3):
                    wait_item(sp, y_ok, at, -3, 2, 2)
                    slot = (at.j - 3) % 2
                    sp.dma_start(y1v[at.img, at.strip(-3)], width_modes[:, slot, :]).then_inc(y_stored[slot], 16)
                if live(at, -2):
                    wait_item(sp, x1_ok, at, -2, 4, 4)
                    slot = (at.j - 2) % RING
                    for i2, ab in PARTS:
                        sp.dma_start(x1v[at.index(-2), ab, :, :, i2, :], xs[:, slot, :, i2, ab, :]).then_inc(stored[slot], 16)

            def image(img, more):
                sweep(sp, img, lambda at: body(at, more), straight=RING)
                join(sp, img, x_stores=True, y_stores=True)

            load(0, 0)
            with sp.Fori(0, IMG - 1) as img:
                image(img, True)
            image(IMG - 1, False)

        @block.tensor
        def _(pe):
            def project(dst, i, at, c):
                flat = lambda x: x[:, (at.j - 1) % 2, CH * c:CH * (c + 1), :].rearrange("p w n -> p (w n)")
                hi, lo = flat(xt_hi), flat(xt_lo)
                nc.tensor.matmul(dst, w_hi[:, i, :], hi, start=True, stop=False)
                nc.tensor.matmul(dst, w_hi[:, i, :], lo, start=False, stop=False)
                return nc.tensor.matmul(dst, w_lo[:, i, :], hi, start=False, stop=True)

            def peak_scores(at, t, u):
                if not live(at, -1, t):
                    return
                wait_item(pe, ops1_ok, at, -1, NC, t + 1)
                wait_item(pe, qd_ok, at, -1, NC, t + 1)
                wait_item(pe, peak_ok, at, -1, NU, UN * t + u)
                for j in range(UP):
                    pair = UP * u + j
                    last = nc.tensor.matmul(peak_bank[:, j * 256:(j + 1) * 256], q_diag[:, t % 2, pair, :],
                                            k_heads[:, t % 2, pair].rearrange("p h n -> p (h n)"),
                                            start=True, stop=True)
                last.then_inc(peak_ps, 1)

            def scores(at, t, u):
                if not live(at, -1, t):
                    return
                unit = UN * t + u
                ps = score_bank[u]
                wait_item(pe, pd_ok, at, -1, NU, unit + 1)
                wait_item(pe, ops2_ok, at, -1, NC, t + 1)
                wait_item(pe, probs_ok, at, -1, NU, unit - 1)
                nc.tensor.matmul(ps[:], neg_same_r[:], peak_diag[:, unit % 4].rearrange("p a h n -> p (a h n)"),
                                 start=True, stop=False)
                for j in range(UP):
                    pair = UP * u + j
                    last = nc.tensor.matmul(ps[:, j * 256:(j + 1) * 256], k_diag[:, t % 4, pair, :],
                                            q_heads[:, t % 4, pair].rearrange("p h n -> p (h n)"),
                                            start=False, stop=(j == UP - 1))
                last.then_inc(score_ps, 1)

            def values(at, t, u):
                if not live(at, -1, t):
                    return
                unit = UN * t + u
                wait_item(pe, probs_ok, at, -1, NU, unit + 1)
                wait_item(pe, vo_ok, at, -1, NC, t + 1)
                wait_item(pe, weighted_ok, at, -1, NU, unit - 1)
                for j in range(UP):
                    for g in range(2):
                        o = (2 * j + g) * P
                        last = nc.tensor.matmul(
                            value_bank[u][:, o:o + P], v_ones[:, t % 4, UP * u + j, g, :],
                            probs[:, unit % 4, j, 2 * g:2 * g + 2, :].rearrange("p h n -> p (h n)"),
                            start=True, stop=True)
                last.then_inc(value_ps, 1)

            def tick(at, c):
                if live(at, -1, c):
                    wait_item(pe, xt_ok, at, -1, NG, NG)
                    wait_item(pe, qk_ok, at, -1, NC, c)
                    project(qk_bank[:, 0:256], 0, at, c)
                    project(qk_bank[:, 256:512], 1, at, c).then_inc(qk_ps, 1)
                peak_scores(at, c - 1, 0)
                scores(at, c - 2, 0)
                if live(at, -1, c):
                    wait_item(pe, vd_ok, at, -1, NC, c)
                    if live(at, 0):
                        wait_item(pe, xt_sum, at, 0, NG, (c + 1) // 2)
                    if live(at, -3):
                        wait_item(pe, y_ok, at, -3, 2, (c >= 4) + (c >= 6))
                    project(mix_bank[:, 0:256], 2, at, c).then_inc(v_ps, 1)
                if c >= NG and live(at, -2):
                    g = c - NG
                    wait_item(pe, heads_ok, at, -2, NU, NU)
                    wait_item(pe, x1_ok, at, -2, NG, g)
                    if live(at, -1, c - 1):
                        wait_item(pe, vo_ok, at, -1, NC, c)
                    for i in range(GRP):
                        tok = heads[:, (at.j - 2) % 2, GRP * g + i].rearrange("p w j -> p (w j)")
                        last = nc.tensor.matmul(out_bank[:, i * P:(i + 1) * P], tok, w_out[:], start=True, stop=True)
                    last.then_inc(out_ps, 1)
                values(at, c - 3, 0)
                peak_scores(at, c - 1, 1)
                if live(at, -1, c):
                    wait_item(pe, vd_ok, at, -1, NC, c + 1)
                    wait_item(pe, vo_ok, at, -1, NC, c)
                    if live(at, -2):
                        wait_item(pe, x1_ok, at, -2, NG, max(c - NG + 1, 0))
                    for j in range(CH):
                        last = nc.tensor.transpose(out_bank[:, j * P:(j + 1) * P], v_diag[:, c % 2, j, :], ident[:])
                    last.then_inc(vt_ps, 1)
                scores(at, c - 2, 1)
                values(at, c - 3, 1)
                if c % 2 == 0 and live(at, 0):
                    g = c // 2
                    if g == 0:
                        pe.wait_ge(loaded[at.j], (at.index(0, RING) + 1) * 64)
                    if live(at, -1):
                        wait_item(pe, vd_ok, at, -1, NC, c + 1)
                    wait_item(pe, xt_sum, at, 0, NG, g)
                    for i in range(GRP):
                        r, i2 = 2 * g + i // 2, i % 2
                        last = nc.tensor.transpose(mix_bank[:, i * P:(i + 1) * P],
                                                   xs[:, at.j, r, i2].rearrange("p a c -> p (a c)"), ident[:])
                    last.then_inc(xt_ps, 1)
                if c in (3, 5) and live(at, -3):
                    half = c // 4
                    wait_item(pe, x_lo, at, -3, NG, 2 * half + 2)
                    wait_item(pe, y_ok, at, -3, 2, half)
                    if live(at, -1):
                        wait_item(pe, vd_ok, at, -1, NC, c + 1)
                    if live(at, 0):
                        wait_item(pe, xt_sum, at, 0, NG, (c + 1) // 2)
                    rows = slice(4 * half, 4 * half + 4)
                    for i in range(4):
                        ab, i2 = i // 2, i % 2
                        nc.tensor.matmul(mix_bank[0:LO + KW, 0:256], fwd_parts[:, i, :], x1_hi[:, rows, i2, ab, :],
                                         start=(i == 0), stop=False)
                        last = nc.tensor.matmul(mix_bank[0:LO + KW, 0:256], fwd_parts[:, i, :], x1_lo[:, rows, i2, ab, :],
                                                start=False, stop=(i == 3))
                    last.then_inc(y_ps, 1)

            def body(at):
                for c in range(NC):
                    tick(at, c)

            pe.wait_ge(consts, CONSTS)
            pe.wait_ge(zeroed, ZEROED)
            with pe.Fori(0, IMG) as img:
                pe.wait_ge(img_set, (img + 1) * SET_STEPS)
                sweep(pe, img, body)
                pe.wait_ge(sum_ok, (img + 1) * (NG * S))
                pe.wait_ge(x_hi, (img + 1) * (NG * S))
                for k in range(GRP):
                    last = nc.tensor.matmul(out_bank[:, 0:1], sum_sq[:, k * P:(k + 1) * P], ones[:],
                                            start=(k == 0), stop=(k == GRP - 1))
                last.then_inc(sum_ps, 1)
                join(pe, img)

        @block.scalar
        def _(act):
            def exponentials(at, t, u):
                if not live(at, -1, t):
                    return
                unit = UN * t + u
                wait_item(act, score_ps, at, -1, NU, unit + 1)
                wait_item(act, value_ps, at, -1, NU, unit - 3)
                nc.scalar.activation(probs[:, unit % 4].rearrange("p a h n -> p (a h n)"), score_bank[u][:], ACT.Exp)\
                    .then_inc(probs_ok, 1)

            def inverse_sums(at, t, u):
                if not live(at, -1, t):
                    return
                unit = UN * t + u
                wait_item(act, value_ps, at, -1, NU, unit + 1)
                wait_item(act, inv_ok, at, -1, NU, unit - 1)
                wait_item(act, weighted_ok, at, -1, NU, unit - 1)
                ps = value_bank[u][:].rearrange("p (a g h n) -> p a g h n", a=UP, g=2, h=2)
                lg, inv = log_sum[:, unit % 2], inv_sum[:, unit % 2]
                flat = lambda x: x.rearrange("p a h n -> p a (h n)")
                nc.scalar.activation(flat(lg[0:64]), flat(ps[64:128, :, 0]), ACT.Ln)
                nc.scalar.activation(flat(lg[64:128]), flat(ps[0:64, :, 1]), ACT.Ln).then_inc(log_ok, 1)
                wait_item(act, log_ok, at, -1, NU, unit + 1)
                for h in range(2):
                    last = nc.scalar.activation(inv[:, :, h], lg[:, :, h], ACT.Exp, bias=other_head[:, h:h + 1], scale=-1.0)
                last.then_inc(inv_ok, 1)

            def tick(at, c):
                if c in (4, 6) and live(at, -3):
                    half = (c - 4) // 2
                    wait_item(act, y_ps, at, -3, 2, half + 1)
                    slot = (at.j - 3) % 2
                    if half == 0 and (at.known is None or at.known >= 5):
                        act.wait_ge(y_stored[slot], at.index(-3, 2) * 16)
                    nc.scalar.activation(width_modes[:, slot, 256 * half:256 * half + 256], mix_bank[0:KW, 0:256],
                                         ACT.Copy).then_inc(y_part, 1)
                inverse_sums(at, c - 4, 1)
                if live(at, -1, c):
                    wait_item(act, qk_ps, at, -1, NC, c + 1)
                    wait_item(act, ops2_ok, at, -1, NC, c - 1)
                    wait_item(act, qd_ok, at, -1, NC, c - 1)
                    flat = lambda x: x.rearrange("p w n -> p (w n)")
                    nc.scalar.activation(flat(q_sb[:, c % 2]), qk_bank[:, 0:256], ACT.Identity, bias=b_q[:])
                    nc.scalar.activation(flat(k_sb[:, c % 2]), qk_bank[:, 256:512], ACT.Identity,
                                         bias=b_in[:, 1:2]).then_inc(qk_ok, 1)
                exponentials(at, c - 2, 0)
                if live(at, -1, c):
                    wait_item(act, v_ps, at, -1, NC, c + 1)
                    wait_item(act, vt_ps, at, -1, NC, c - 1)
                    src = mix_bank[:, 0:256].rearrange("p (w n) -> p w n", n=N)
                    nc.scalar.activation(v_diag[0:64, c % 2, :, 0:64], src[0:64], ACT.Identity, bias=b_in[0:64, 2:3])
                    nc.scalar.activation(v_diag[64:128, c % 2, :, 64:128], src[64:128], ACT.Identity,
                                         bias=b_in[64:128, 2:3]).then_inc(vd_ok, 1)
                if c < NG and live(at, -3):
                    wait_item(act, x1_ok, at, -3, NG, NG)
                    wait_item(act, y_ps, at, -3, 2, c // 2 - 1)
                    flat = lambda x: x.rearrange("p r i a c -> p (r i a c)")
                    nc.scalar.activation(flat(x1_hi[:, 2 * c:2 * c + 2]), flat(xs[:, (at.j - 3) % RING, 2 * c:2 * c + 2]),
                                         ACT.Copy).then_inc(x_hi, 1)
                inverse_sums(at, c - 3, 0)
                if live(at, -1, c):
                    wait_item(act, vt_ps, at, -1, NC, c + 1)
                    wait_item(act, value_ps, at, -1, NU, UN * (c - 3))
                    src = out_bank[:].rearrange("p (w ab g k) -> p w ab g k", w=CH, ab=2, g=2)
                    for g in range(2):
                        dst = v_ones[:, c % 4, :, g, 64 * g:64 * g + 64].rearrange("p w (ab k) -> p w ab k", ab=2)
                        last = nc.scalar.activation(dst, src[:, :, :, g, :], ACT.Copy)
                    last.then_inc(vo_ok, 1)
                exponentials(at, c - 2, 1)
                if live(at, -3) and 2 <= c < 6:
                    q = c - 2
                    wait_item(act, x1_ok, at, -3, NG, NG)
                    wait_item(act, sum_ok, at, -3, NG, q - 1)
                    nc.scalar.activation(sq[:, q % 2, :], xs[:, (at.j - 3) % RING, 2 * q:2 * q + 2].rearrange("p r i a c -> p (r i a c)"),
                                         ACT.Square).then_inc(sq_ok, 1)

            def body(at):
                for c in range(NC):
                    tick(at, c)

            act.wait_ge(consts, CONSTS)
            act.wait_ge(zeroed, ZEROED)
            nc.scalar.preload_act_table_set("natural_log_exp_and_others")
            with act.Fori(0, IMG) as img:
                act.wait_ge(img_set, (img + 1) * SET_STEPS)
                sweep(act, img, body)
                join(act, img, y_stores=True)

        @block.vector
        def _(dve):
            def maximum(at, t, u):
                if not live(at, -1, t):
                    return
                unit = UN * t + u
                wait_item(dve, peak_ps, at, -1, NU, unit + 1)
                nc.vector.tensor_reduce(peak[:, unit % 2, :], peak_bank[:].rearrange("p (a n) -> p a n", n=N),
                                        axis=AX.X, op=ALU.max).then_inc(peak_ok, 1)
                wait_item(dve, peak_ok, at, -1, NU, unit + 1)
                wait_item(dve, score_ps, at, -1, NU, unit - 3)
                nc.vector.tensor_tensor(
                    peak_diag[:, unit % 4].rearrange("p a h n -> p (a h) n"),
                    token_eye[:].unsqueeze(1).to_broadcast([P, UP * NH, N]),
                    peak[:, unit % 2, :].unsqueeze(2).to_broadcast([P, UP * NH, N]), ALU.mult).then_inc(pd_ok, 1)

            def normalise(at, t, u):
                if not live(at, -1, t):
                    return
                unit = UN * t + u
                wait_item(dve, inv_ok, at, -1, NU, unit + 1)
                ps = value_bank[u][:].rearrange("p (a g h n) -> p a g h n", a=UP, g=2, h=2)
                slot = unit % 2
                for g in range(2):
                    rows = slice(64 * g, 64 * g + 64)
                    last = nc.vector.tensor_tensor(weighted[rows, slot], ps[rows, :, g], inv_sum[rows, slot], ALU.mult)
                last.then_inc(weighted_ok, 1)
                wait_item(dve, weighted_ok, at, -1, NU, unit + 1)
                if t == 0 and u == 0:
                    wait_item(dve, out_ps, at, -3, NG, NG)
                w = CH * (t % NC) + UP * u
                ring = (at.j - 1 if t >= 0 else at.j - 2) % 2
                one = lambda h: weighted[:, slot, :, h].rearrange("p a (k j) -> p a k j", j=4)
                nc.vector.tensor_tensor(heads[:, ring, :, w:w + UP, :].rearrange("p k a j -> p a k j"),
                                        one(0), one(1), ALU.add).then_inc(heads_ok, 1)

            def tick(at, c):
                if c in (4, 6) and live(at, -3):
                    half = (c - 4) // 2
                    wait_item(dve, y_part, at, -3, 2, half + 1)
                    modes = width_modes[:, (at.j - 3) % 2, 256 * half:256 * half + 256]
                    nc.vector.tensor_tensor(modes, mix_bank[LO:LO + KW, 0:256], modes, ALU.add).then_inc(y_ok, 1)
                maximum(at, c - 1, 0)
                normalise(at, c - 4, 1)
                if c >= NG and live(at, -2):
                    g = c - NG
                    wait_item(dve, out_ps, at, -2, NG, g + 1)
                    row = xs[:, (at.j - 2) % RING, 2 * g:2 * g + 2].rearrange("p r i a c -> p (r i a c)")
                    nc.vector.tensor_tensor(row, out_bank[:], row, ALU.add).then_inc(x1_ok, 1)
                if live(at, -1, c):
                    wait_item(dve, qk_ok, at, -1, NC, c + 1)
                    wait_item(dve, peak_ps, at, -1, NU, UN * (c - 1))
                    for ab in range(2):
                        last = nc.vector.tensor_scalar(q_diag[:, c % 2, :, 64 * ab:64 * ab + 64], q_sb[:, c % 2],
                                                       half_mask[:, ab:ab + 1], None, ALU.mult)
                    last.then_inc(qd_ok, 1)
                if c % 2 and live(at, 0):
                    g = c // 2
                    hi, lo = (x[:, at.j % 2].rearrange("p w (k j) -> p w k j", j=4)[:, :, GRP * g:GRP * (g + 1)]
                              for x in (xt_hi, xt_lo))
                    wait_item(dve, xt_sum, at, 0, NG, g + 1)
                    nc.vector.tensor_copy(hi, xt[:]).then_inc(xt_part, 1)
                    wait_item(dve, xt_part, at, 0, NG, g + 1)
                    nc.vector.tensor_tensor(lo, xt[:], hi.bitcast(F32), ALU.subtract).then_inc(xt_ok, 1)
                maximum(at, c - 1, 1)
                normalise(at, c - 3, 0)
                if c % 2 == 0 and live(at, 0):
                    g = c // 2
                    wait_item(dve, xt_ps, at, 0, NG, g + 1)
                    wait_item(dve, xt_ok, at, 0, NG, g)
                    add = mod_cur[:].rearrange("p (k j) -> p k j", j=4)[:, GRP * g:GRP * (g + 1), :]
                    nc.vector.tensor_tensor(xt[:].rearrange("p w k j -> p k w j"),
                                            mix_bank[:].rearrange("p (k w j) -> p k w j", k=GRP, j=4),
                                            add.unsqueeze(2).to_broadcast([P, GRP, WP, 4]), ALU.add).then_inc(xt_sum, 1)

            def body(at):
                for c in range(NC):
                    tick(at, c)

            nc.vector.memset(v_diag[:], 0.0).then_inc(zeroed, 1)
            nc.vector.memset(v_ones[:], 0.0).then_inc(zeroed, 1)
            nc.vector.memset(fwd_parts[:].bitcast(F32), 0.0).then_inc(zeroed, 1)
            dve.wait_ge(zeroed, 3)
            for ab in range(2):
                for g in range(2):
                    o = 64 * (1 - g) + 32 * ab
                    nc.vector.memset(v_ones[64 * ab:64 * ab + 64, :, :, g, o:o + 32], 1.0).then_inc(zeroed, 1)
            dve.wait_ge(consts, CONSTS)
            nc.vector.tensor_copy(fwd_parts[:, :, 0:KW], fwd_w[:]).then_inc(zeroed, 1)
            dve.wait_ge(zeroed, 8)
            nc.vector.tensor_tensor(fwd_parts[:, :, LO:LO + KW], fwd_w[:], fwd_parts[:, :, 0:KW].bitcast(F32), ALU.subtract)\
                .then_inc(zeroed, 1)
            nc.vector.tensor_copy(neg_same_r[:], neg_same[:]).then_inc(zeroed, 1)
            nc.vector.tensor_scalar(b_q[:], b_in[:, 0:1], float(HD) ** -0.5, None, ALU.mult).then_inc(zeroed, 1)

            with dve.Fori(0, IMG) as img:
                st = stats1[:, img, :]
                for i in range(3):
                    nc.vector.tensor_scalar(w_cur[:, i, :], w_in[:, i, :], st[:, 2:3],
                                            float(HD) ** -0.5 if i == 0 else 1.0, ALU.mult, ALU.mult).then_inc(img_set, 1)
                nc.vector.tensor_scalar(mod_cur[:], mod[:], st[:, 1:2], st[:, 0:1], ALU.mult, ALU.subtract)\
                    .then_inc(img_set, 1)
                nc.vector.memset(sum_sq[:], 0.0).then_inc(img_set, 1)
                dve.wait_ge(img_set, img * SET_STEPS + 5)
                nc.vector.tensor_copy(w_hi[:], w_cur[:]).then_inc(img_set, 1)
                dve.wait_ge(img_set, img * SET_STEPS + 6)
                nc.vector.tensor_tensor(w_lo[:], w_cur[:], w_hi[:].bitcast(F32), ALU.subtract).then_inc(img_set, 1)
                dve.wait_ge(img_set, (img + 1) * SET_STEPS)
                sweep(dve, img, body)
                dve.wait_ge(sum_ps, img + 1)
                nc.vector.tensor_copy(sqsum[:, bass.ds(img, 1)], out_bank[:, 0:1]).then_inc(img_done, 1)
                join(dve, img)

        @block.gpsimd
        def _(pool):
            def tick(at, c):
                if live(at, -1, c):
                    q, k = q_sb[:, c % 2], k_sb[:, c % 2]
                    wait_item_apart(pool, peak_ps, at, -1, NU, UN * (c - 1), passed)
                    wait_item_apart(pool, qk_ok, at, -1, NC, c + 1, passed)
                    for h in range(NH):
                        last = nc.gpsimd.tensor_scalar(k_heads[:, c % 2, :, h, :], k, head_mask[:, h:h + 1], 1.0,
                                                       ALU.mult, ALU.mult)
                    last.then_inc(ops1_ok, 1)
                    wait_item_apart(pool, score_ps, at, -1, NU, UN * (c - 3), passed)
                    for h in range(NH):
                        nc.gpsimd.tensor_scalar(q_heads[:, c % 4, :, h, :], q, head_mask[:, h:h + 1], 1.0, ALU.mult, ALU.mult)
                    for ab in range(2):
                        last = nc.gpsimd.tensor_scalar(k_diag[:, c % 4, :, 64 * ab:64 * ab + 64], k,
                                                       half_mask[:, ab:ab + 1], 1.0, ALU.mult, ALU.mult)
                    last.then_inc(ops2_ok, 1)
                if live(at, -3) and 1 <= c < 5:
                    q = c - 1
                    wait_item(pool, x_hi, at, -3, NG, q + 1)
                    part = lambda x: x[:, 2 * q:2 * q + 2].rearrange("p r i a c -> p (r i a c)")
                    nc.gpsimd.tensor_tensor(part(x1_lo), part(xs[:, (at.j - 3) % RING]), part(x1_hi).bitcast(F32), ALU.subtract)\
                        .then_inc(x_lo, 1)
                if live(at, -3) and 3 <= c < 7:
                    q = c - 3
                    wait_item(pool, sq_ok, at, -3, NG, q + 1)
                    wait_item(pool, sum_ok, at, -3, NG, q)
                    nc.gpsimd.tensor_tensor(sum_sq[:], sum_sq[:], sq[:, q % 2, :], ALU.add).then_inc(sum_ok, 1)

            def body(at):
                for c in range(NC):
                    tick(at, c)

            pool.wait_ge(consts, CONSTS)
            pool.wait_ge(zeroed, ZEROED)
            with pool.Fori(0, IMG) as img:
                pool.wait_ge(img_set, (img + 1) * SET_STEPS)
                sweep(pool, img, body)
                join(pool, img)


CONSTS = 11 * 16
ZEROED = 11
SET_STEPS = 7


def pass3(nc, ext, y1, sqsum, group_avg, back, IMG, H):
    HB = min(P, H)
    HQ = H // HB
    IC = 2 * IMG
    WR = 4
    NB = 8
    PARTS = [(n, min(n + NB, M2)) for n in range(0, M2, NB)]
    yv = y1.rearrange("i k (q p c) -> i q p k c", q=HQ, p=HB)
    with ExitStack() as c:
        sb = lambda n, shape, dt=F32: c.enter_context(nc.sbuf_tensor(n, shape, dt))
        yt = sb("yt", [HB, 2, HQ, KW, C])
        fwd_h = sb("fwd_h", [HB, HQ, 2, 2 * M1])
        ident = sb("p3_ident", [P, P])
        mode_parts = sb("mode_parts", [2 * M1, P])
        group_mean2 = sb("group_mean2", [P, P])
        modes = sb("modes", [2 * M1, M2, C])
        dc = sb("dc", [P, 1])
        bias = sb("bias", [P, 1])
        square = sb("square", [P, 1])
        stats = sb("p3_stats", [P, 3])
        work = sb("p3_work", [P, 3])
        shift = sb("shift", [P, 1])
        ready = sb("p3_ready", [P, 2])
        mixed_in = sb("mixed_in", [P, M1, M2, IC])
        col = sb("col", [P, WR, M2, IC])
        wt = sb("wt", [P, WR, M2, C])
        mixed = sb("mixed", [C, IMG, M2, 2, M1])
        mixed_img = sb("mixed_img", [C, M2, 2 * M1])
        bank = lambda n: c.enter_context(nc.psum_tensor(n, [P, 512], F32))
        h_bank, t_bank, m_bank = [[bank(f"p3_{k}{i}") for i in range(2)] for k in ("h", "t", "m")]
        stat_bank = bank("p3_stat")
        sem = lambda n: c.enter_context(nc.semaphore(n))
        consts, cleared, bias_ok = sem("p3_consts"), sem("p3_cleared"), sem("p3_bias_ok")
        y_ok = [sem(f"p3_y_ok{i}") for i in range(2)]
        h_ps, h_ok = sem("p3_h_ps"), sem("p3_h_ok")
        dc_ps, dc_ok, avg = sem("p3_dc_ps"), sem("p3_dc_ok"), sem("p3_avg")
        chain, dev, shift_ok = sem("p3_chain"), sem("p3_dev"), sem("p3_shift")
        t_ps, t_ok, fixed = sem("p3_t_ps"), sem("p3_t_ok"), sem("p3_fixed")
        w_ok = [sem(f"p3_w{i}") for i in range(WR)]
        col_ok, m_ps, m_ok = sem("p3_col_ok"), sem("p3_m_ps"), sem("p3_m_ok")
        i_ok, b_ps, b_ok = sem("p3_i_ok"), sem("p3_b_ps"), sem("p3_b_ok")
        passed = sem("p3_passed")
        NP_ = len(PARTS)
        wv = ext["w_mix"].rearrange("m p (n o) -> m p n o", n=M2)
        block = c.enter_context(nc.Block())

        @block.sync
        def _(sp):
            for dst, name in ((ident, "ident"), (mode_parts, "mode_parts"), (group_mean2, "group_mean2"), (bias, "b_out")):
                sp.dma_start(dst[:], ext[name]).then_inc(consts, 16)
            sp.dma_start(fwd_h[:].rearrange("p q a m -> p (q a m)"), ext["fwd_h"]).then_inc(consts, 16)
            for img in range(IMG):
                if img >= 2:
                    sp.wait_ge(h_ps, (img - 1) * NP_)
                for q in range(HQ):
                    sp.dma_start(yt[:, img % 2, q], yv[img, q]).then_inc(y_ok[img % 2], 16)
            for i in range(WR):
                sp.dma_start(wt[:, i], wv[i]).then_inc(w_ok[i], 16)
            with sp.Fori(1, M1 // WR) as quad:
                for i in range(WR):
                    sp.wait_ge(m_ps, quad * WR + (i - WR + 1))
                    sp.dma_start(wt[:, i], wv[quad * WR + i]).then_inc(w_ok[i], 16)

        @block.tensor
        def _(pe):
            def image(pair, slot):
                img = pair * 2 + slot
                pe.wait_ge(y_ok[slot], (pair + 1) * (16 * HQ))
                for k, (n0, n1) in enumerate(PARTS):
                    ps = h_bank[k % 2]
                    if k >= 2:
                        pe.wait_ge(h_ok, img * NP_ + (k - 1))
                    w = (n1 - n0) * C
                    for q in range(HQ):
                        for part in range(2):
                            last = nc.tensor.matmul(
                                ps[0:2 * M1, 0:w], fwd_h[:, q, part, :],
                                yt[:, slot, q, part * M2 + n0:part * M2 + n1, :].rearrange("p n c -> p (n c)"),
                                start=(q == 0 and part == 0), stop=(q == HQ - 1 and part == 1))
                    last.then_inc(h_ps, 1)
                wait_apart(pe, h_ok, (img + 1) * NP_, passed)
                for half in range(2):
                    last = nc.tensor.matmul(stat_bank[64 * half:64 * half + 64, 4:5], modes[:, 0, :],
                                            ident[0:2 * M1, M1 // 2:M1 // 2 + 1], start=True, stop=True)
                last.then_inc(dc_ps, 1)
                pe.wait_ge(dc_ok, 4 * img + 4)
                nc.tensor.matmul(stat_bank[:, 0:1], group_mean2[:], dc[:], start=True, stop=True)
                nc.tensor.matmul(stat_bank[:, 1:2], group_avg[:], work[:, 2:3], start=True, stop=True).then_inc(avg, 1)
                for k, (n0, n1) in enumerate(PARTS):
                    if k >= 2:
                        wait_apart(pe, t_ok, img * NP_ + (k - 1), passed)
                    for n in range(n0, n1):
                        for half in range(2):
                            last = nc.tensor.matmul(
                                t_bank[k % 2][64 * half:64 * half + 64, (n - n0) * 64:(n - n0 + 1) * 64],
                                modes[:, n, :], mode_parts[:, 64 * half:64 * half + 64], start=True, stop=True)
                    last.then_inc(t_ps, 1)
                pe.wait_ge(fixed, 2 * img + 2)

            pe.wait_ge(consts, 80)
            with pe.Fori(0, IMG // 2) as pair:
                for slot in range(2):
                    image(pair, slot)
            with pe.Fori(0, M1 // WR) as quad:
                for i in range(WR):
                    pe.wait_ge(w_ok[i], (quad + 1) * 16)
                    pe.wait_ge(col_ok, quad * WR + (i + 1))
                    pe.wait_ge(m_ok, quad * WR + (i + 1))
                    for n in range(M2):
                        last = nc.tensor.matmul(m_bank[i % 2][0:C, n * IC:(n + 1) * IC], wt[:, i, n, :],
                                                col[:, i, n, :], start=True, stop=True)
                    last.then_inc(m_ps, 1)
            with pe.Fori(0, IMG) as img:
                pe.wait_ge(i_ok, img + 1)
                for k, (n0, n1) in enumerate(PARTS):
                    wait_apart(pe, b_ok, img * NP_ + (k + 1), passed)
                    for n in range(n0, n1):
                        for half in range(2):
                            last = nc.tensor.matmul(
                                h_bank[k % 2][64 * half:64 * half + 64, (n - n0) * C:(n - n0 + 1) * C],
                                mixed_img[:, n, :], ident[0:C, 0:C], start=True, stop=True)
                    last.then_inc(b_ps, 1)

        @block.scalar
        def _(act):
            with act.Fori(0, IMG) as img:
                for k, (n0, n1) in enumerate(PARTS):
                    act.wait_ge(h_ps, img * NP_ + (k + 1))
                    nc.scalar.activation(modes[:, n0:n1, :].rearrange("p n c -> p (n c)"),
                                         h_bank[k % 2][0:2 * M1, 0:(n1 - n0) * C], ACT.Copy).then_inc(h_ok, 1)
                act.wait_ge(chain, img * 4 + 3)
                nc.scalar.activation(stats[:, 1:2], work[:, 2:3], ACT.Sqrt).then_inc(dev, 1)
                act.wait_ge(fixed, img * 2 + 2)
            with act.Fori(0, M1 // WR) as quad:
                for i in range(WR):
                    act.wait_ge(m_ps, quad * WR + (i + 1))
                    nc.scalar.activation(mixed[:, :, :, :, quad * WR + i].rearrange("p i n r -> p n r i"),
                                         m_bank[i % 2][0:C, 0:M2 * IC].rearrange("p (n r i) -> p n r i", n=M2, r=2),
                                         ACT.Copy).then_inc(m_ok, 1)

        @block.vector
        def _(dve):
            nc.vector.memset(back[:], 0.0).then_inc(cleared, 1)
            dve.wait_ge(consts, 80)
            nc.vector.memset(ready[:, 0:1], 0.0).then_inc(m_ok, 2)
            nc.vector.memset(ready[:, 1:2], 0.0).then_inc(b_ok, 2)
            with dve.Fori(0, IMG) as img:
                dve.wait_ge(dc_ps, img + 1)
                nc.vector.tensor_scalar(dc[:], stat_bank[:, 4:5], bias[:], None, ALU.add).then_inc(dc_ok, 1)
                dve.wait_ge(dc_ok, 4 * img + 1)
                nc.vector.tensor_tensor(square[:], stat_bank[:, 4:5], dc[:], ALU.add).then_inc(dc_ok, 1)
                dve.wait_ge(dc_ok, 4 * img + 2)
                nc.vector.tensor_scalar(square[:], square[:], bias[:], H * W / 2.0, ALU.mult, ALU.mult).then_inc(dc_ok, 1)
                dve.wait_ge(dc_ok, 4 * img + 3)
                nc.vector.tensor_tensor(work[:, 2:3], sqsum[:, bass.ds(img, 1)], square[:], ALU.add).then_inc(dc_ok, 1)
                dve.wait_ge(avg, img + 1)
                group_stats(nc, dve, stats, stat_bank, work, chain, img * 4, dev, img)
                nc.vector.tensor_scalar(shift[:], stats[:, 0:1], bias[:], stats[:, 2:3], ALU.subtract, ALU.mult)\
                    .then_inc(shift_ok, 1)
                for k, (n0, n1) in enumerate(PARTS):
                    dve.wait_ge(t_ps, img * NP_ + (k + 1))
                    src = t_bank[k % 2][:, 0:(n1 - n0) * 64].rearrange("p (n r m) -> p n r m", r=2, m=M1)
                    cols = mixed_in[:, :, n0:n1, :].rearrange("p m n (r i) -> p n r m i", r=2)
                    nc.vector.tensor_scalar(cols[:, :, :, :, img], src, stats[:, 2:3], None, ALU.mult).then_inc(t_ok, 1)
                dve.wait_ge(t_ok, (img + 1) * NP_)
                dve.wait_ge(shift_ok, img + 1)
                for half in range(2):
                    rows = slice(64 * half, 64 * half + 64)
                    at = mixed_in[rows, M1 // 2, 0:1, :].rearrange("p n (r i) -> p n r i", r=2)[:, :, half, img]
                    nc.vector.tensor_scalar(at, at, shift[rows, :], None, ALU.subtract).then_inc(fixed, 1)
                dve.wait_ge(fixed, img * 2 + 2)
            with dve.Fori(0, M1 // WR) as quad:
                for i in range(WR):
                    dve.wait_ge(m_ok, quad * WR + (i + 1))
                    nc.vector.tensor_copy(col[:, i].rearrange("p n i -> p (n i)"),
                                          mixed_in[:, quad * WR + i].rearrange("p n i -> p (n i)")).then_inc(col_ok, 1)
            dve.wait_ge(m_ok, M1 + 2)
            dve.wait_ge(cleared, 1)
            nc.vector.tensor_scalar(mixed[:, :, 0, 0, M1 // 2], mixed[:, :, 0, 0, M1 // 2], bias[0:C], None, ALU.add)\
                .then_inc(bias_ok, 1)
            dve.wait_ge(bias_ok, 1)
            with dve.Fori(0, IMG) as img:
                nc.vector.tensor_copy(mixed_img[:].rearrange("p n m -> p (n m)"),
                                      mixed[:, img].rearrange("p n r m -> p (n r m)")).then_inc(i_ok, 1)
                for k, (n0, n1) in enumerate(PARTS):
                    dve.wait_ge(b_ps, img * NP_ + (k + 1))
                    for half in range(2):
                        rows = slice(64 * half, 64 * half + 64)
                        last = nc.vector.tensor_copy(
                            back[rows, img, :, half * M2 + n0:half * M2 + n1].rearrange("p c n -> p n c"),
                            h_bank[k % 2][rows, 0:(n1 - n0) * C].rearrange("p (n c) -> p n c", c=C))
                    last.then_inc(b_ok, 1)


def pass4(nc, ext, x1, back, out, IMG, H):
    HB = min(P, H)
    HQ = H // HB
    SB = HB // PS
    CG = 512 // HB
    GC = C // CG
    TB = 8
    LO = 64
    xv = x1.rearrange("(g r) (p e) -> g p r e", r=PS, p=P)
    ov = out.rearrange("(g r) (p e) -> g p r e", r=PS, p=P)
    with ExitStack() as c:
        sb = lambda n, shape, dt=F32: c.enter_context(nc.sbuf_tensor(n, shape, dt))
        inv_h = sb("inv_h", [P, H])
        inv_w = sb("inv_w", [LO + KW, 4, P])
        w_hi = sb("p4_w_hi", [LO + KW, 4, P], F32R)
        w_lo = sb("p4_w_lo", [KW, 4, P], F32R)
        lines = sb("lines", [LO + KW, HB, C], F32R)
        now = sb("now", [P, C, KW])
        tile = sb("p4_x", [P, TB, PS, 4, C])
        ready = sb("p4_ready", [P, 2])
        bank = lambda n: c.enter_context(nc.psum_tensor(n, [P, 512], F32))
        l_bank = [bank(f"p4_l{i}") for i in range(2)]
        y_bank = [bank(f"p4_y{i}") for i in range(4)]
        sem = lambda n: c.enter_context(nc.semaphore(n))
        consts, zeroed, w_ok = sem("p4_consts"), sem("p4_zeroed"), sem("p4_w_ok")
        now_ok = sem("p4_now_ok")
        loaded = [sem(f"p4_loaded{i}") for i in range(TB)]
        stored = [sem(f"p4_stored{i}") for i in range(TB)]
        l_ps, hi_ok, l_ok = sem("p4_l_ps"), sem("p4_hi_ok"), sem("p4_l_ok")
        y_ps, y_ok = sem("p4_y_ps"), sem("p4_y_ok")
        passed = sem("p4_passed")
        block = c.enter_context(nc.Block())
        STRIPS = IMG * H // PS

        @block.sync
        def _(sp):
            sp.dma_start(inv_h[:], ext["inv_h"]).then_inc(consts, 16)
            sp.wait_ge(zeroed, 2)
            for row in (0, LO):
                sp.dma_start(inv_w[row:row + KW].rearrange("k i p -> k (i p)"), ext["inv_w"]).then_inc(consts, 16)
            for t in range(TB):
                sp.dma_start(tile[:, t].rearrange("p r i c -> p r (i c)"), xv[t]).then_inc(loaded[t], 16)
            with sp.Fori(0, STRIPS // TB - 1) as i:
                for t in range(TB):
                    sp.wait_ge(y_ok, (i * TB + (t + 2)) * 4)
                    sp.dma_start(ov[i * TB + t], tile[:, t].rearrange("p r i c -> p r (i c)")).then_inc(stored[t], 16)
                    if t:
                        sp.wait_ge(stored[t - 1], (i + 1) * 16)
                        sp.dma_start(tile[:, t - 1].rearrange("p r i c -> p r (i c)"), xv[i * TB + (TB + t - 1)])\
                            .then_inc(loaded[t - 1], 16)
                sp.wait_ge(stored[TB - 1], (i + 1) * 16)
                sp.dma_start(tile[:, TB - 1].rearrange("p r i c -> p r (i c)"), xv[i * TB + (2 * TB - 1)])\
                    .then_inc(loaded[TB - 1], 16)
            for t in range(TB):
                sp.wait_ge(y_ok, (STRIPS - TB + t + 2) * 4)
                sp.dma_start(ov[STRIPS - TB + t], tile[:, t].rearrange("p r i c -> p r (i c)")).then_inc(stored[t], 16)
            for t in range(TB):
                sp.wait_ge(stored[t], (STRIPS // TB) * 16)

        @block.tensor
        def _(pe):
            pe.wait_ge(consts, 48)
            pe.wait_ge(w_ok, 2)
            with pe.Fori(0, IMG) as img:
                wait_apart(pe, now_ok, img + 1, passed)
                with pe.Fori(0, HQ) as hq:
                    blk = img * HQ + hq
                    for g in range(GC):
                        wait_apart(pe, l_ok, blk * GC + (g + 1), passed)
                        for i in range(CG):
                            last = nc.tensor.matmul(l_bank[g % 2][0:KW, i * HB:(i + 1) * HB], now[:, g * CG + i, :],
                                                    inv_h[:, bass.ds(hq * HB, HB)], start=True, stop=True)
                        last.then_inc(l_ps, 1)
                    wait_apart(pe, l_ok, blk * GC + (GC + 2), passed)
                    with pe.Fori(0, SB // 2) as s:
                        for t in range(2):
                            for i in range(4):
                                q = 4 * t + i
                                wait_apart(pe, y_ok, (blk * SB + s * 2) * 4 + (q + 1), passed)
                                at = lines[:, bass.ds(s * (2 * PS) + t * PS, PS), :].rearrange("k r c -> k (r c)")
                                nc.tensor.matmul(y_bank[q % 4][:], w_hi[:, i, :], at, start=True, stop=False)
                                nc.tensor.matmul(y_bank[q % 4][:], w_lo[:, i, :], at[0:KW], start=False, stop=True)\
                                    .then_inc(y_ps, 1)

        @block.scalar
        def _(act):
            act.wait_ge(zeroed, 2)
            with act.Fori(0, IMG * HQ) as blk:
                for g in range(GC):
                    act.wait_ge(l_ps, blk * GC + (g + 1))
                    if g == 0:
                        act.wait_ge(y_ok, blk * (4 * SB) + 4)
                    nc.scalar.activation(lines[0:KW, :, g * CG:(g + 1) * CG].rearrange("k h c -> k c h"),
                                         l_bank[g % 2][0:KW, :].rearrange("k (c h) -> k c h", c=CG), ACT.Copy)\
                        .then_inc(hi_ok, 1)

        @block.vector
        def _(dve):
            nc.vector.memset(inv_w[:], 0.0).then_inc(zeroed, 1)
            nc.vector.memset(lines[32:LO].bitcast(F32), 0.0).then_inc(zeroed, 1)
            nc.vector.memset(ready[:, 0:1], 0.0).then_inc(l_ok, 2)
            nc.vector.memset(ready[:, 1:2], 0.0).then_inc(y_ok, 4)
            dve.wait_ge(consts, 48)
            nc.vector.tensor_copy(w_hi[:], inv_w[:]).then_inc(w_ok, 1)
            dve.wait_ge(w_ok, 1)
            nc.vector.tensor_tensor(w_lo[:], inv_w[0:KW], w_hi[0:KW].bitcast(F32), ALU.subtract).then_inc(w_ok, 1)
            with dve.Fori(0, IMG) as img:
                dve.wait_ge(l_ok, img * (HQ * GC) + 2)
                nc.vector.tensor_copy(now[:].rearrange("p c k -> p (c k)"),
                                      back[:, img].rearrange("p c k -> p (c k)")).then_inc(now_ok, 1)
                with dve.Fori(0, HQ) as hq:
                    blk = img * HQ + hq
                    for g in range(GC):
                        dve.wait_ge(hi_ok, blk * GC + (g + 1))
                        hi, lo = (lines[row:row + KW, :, g * CG:(g + 1) * CG].rearrange("k h c -> k c h") for row in (0, LO))
                        nc.vector.tensor_tensor(lo, l_bank[g % 2][0:KW, :].rearrange("k (c h) -> k c h", c=CG),
                                                hi.bitcast(F32), ALU.subtract).then_inc(l_ok, 1)
                    with dve.Fori(0, SB // TB) as s:
                        ring = blk * (SB // TB) + s
                        for t in range(TB):
                            dve.wait_ge(loaded[t], (ring + 1) * 16)
                            for i in range(4):
                                dve.wait_ge(y_ps, (ring * TB + t) * 4 + (i + 1))
                                at = tile[:, t, :, i, :]
                                nc.vector.tensor_tensor(at, y_bank[i][:].rearrange("p (r c) -> p r c", c=C), at, ALU.add)\
                                    .then_inc(y_ok, 1)


def block_diagonal(a, b):
    m = np.zeros((a.shape[0] + b.shape[0], a.shape[1] + b.shape[1]), a.dtype)
    m[:a.shape[0], :a.shape[1]] = a
    m[a.shape[0]:, a.shape[1]:] = b
    return m


def layout(x, modulator, w_qkv, b_qkv, w_proj, b_proj, w_real, w_imag):
    a = {"x": x.reshape(-1, W * C)}
    parts = [w_qkv[i * C:(i + 1) * C].T for i in range(3)]
    a["w_in"] = np.stack([block_diagonal(w, w) for w in parts], 1)
    a["b_in"] = np.stack([np.concatenate([b, b]) for b in b_qkv.reshape(3, C)], 1)
    m = modulator.reshape(PS, 4, 2, C).transpose(3, 0, 2, 1).reshape(C, N)
    a["mod"] = np.concatenate([m, m])
    w = w_proj.T.reshape(2, 2, HD, C)
    o = np.zeros((2, 2, 2, HD, 2, C), w_proj.dtype)
    for ab in range(2):
        o[:, ab, :, :, ab, :] = w
    a["w_out"] = o.reshape(P, P)
    a["b_out"] = np.concatenate([b_proj, b_proj]).reshape(P, 1)
    a["w_mix"] = np.stack([w_real, w_imag], 1).transpose(0, 1, 3, 2, 4).reshape(M1, P, M2 * C)
    return {k: np.ascontiguousarray(v) for k, v in a.items()}


_OUT = ((4, 512, 512, 64), "float32")


def kernel(**inputs):
    import concourse.bacc as _bacc
    from concourse.bass_utils import run_bass_kernel_spmd as _run

    f = {k: np.asarray(v) for k, v in inputs.items()}
    x = f["x"]
    arrays = layout(x, f["L0_conv_modulator"], f["L0_conv_w_qkv"], f["L0_conv_b_qkv"], f["L0_conv_w_proj"],
                    f["L0_conv_b_proj"], f["L1_conv_W_real"], f["L1_conv_W_imag"])
    arrays.update(tables(x.shape[1]))
    nc = _bacc.Bacc("TRN2", target_bir_lowering=False, num_devices=1)
    ext = {k: nc.dram_tensor(f"in_{k}", v.shape, mybir.dt.from_np(v.dtype), kind="ExternalInput").ap()
           for k, v in arrays.items()}
    out = nc.dram_tensor("out", (x.shape[0] * x.shape[1], W * C), F32, kind="ExternalOutput").ap()
    program(nc, ext, out, x.shape[0], x.shape[1])
    r = _run(nc, [{f"in_{k}": v for k, v in arrays.items()}], core_ids=[0])
    return r.results[0]["out"].reshape(x.shape)
```
